# Optimizing a Trainium2 kernel written in Bass

```python
import numpy as np
import jax
import jax.numpy as jnp

def _softmax(x, axis=-1):
    return jax.nn.softmax(x, axis=axis)

def _gelu(x):
    return jax.nn.gelu(x, approximate=True)

def _silu(x):
    return jax.nn.silu(x)

def _sigmoid(x):
    return jax.nn.sigmoid(x)

def _layernorm(x, axis=-1, eps=1e-05):
    m = jnp.mean(x, axis=axis, keepdims=True)
    v = jnp.var(x, axis=axis, keepdims=True)
    return (x - m) / jnp.sqrt(v + eps)

def _scatter_add(tgt, idx, src, axis=0):
    return tgt.at[idx].add(src)

def _segment_sum(src, seg, n):
    return jax.ops.segment_sum(src, seg, n)
kernel_name = 'mk_xattn_seq_d2_seqx_r8_1e7703'

def setup_inputs(seed: int=0):
    np.random.seed(seed)
    _w = jnp.asarray

    def _rec_inputs():
        import jax
        import jax.numpy as jnp
        _rk = jax.random.key(seed)
        x = 7.22e-05 + 1 * jax.random.normal(jax.random.fold_in(_rk, 1), (32, 64, 256), jnp.float32)
        _lenS = 64 - jax.random.randint(jax.random.fold_in(_rk, 7), (32,), 0, max(1, 64 // 4) + 1, jnp.int32)
        _lenS2 = 64 - jax.random.randint(jax.random.fold_in(_rk, 8), (32,), 0, max(1, 64 // 4) + 1, jnp.int32)
        _ctx_2048P = jax.random.normal(jax.random.fold_in(_rk, 11), (32, 16, 256), jnp.float32)
        _ctx_2048c = jax.random.dirichlet(jax.random.fold_in(_rk, 511), 0.3 * jnp.ones((16,), jnp.float32), (32, 64))
        _ctx_2048t = jnp.einsum('bsk,bkd->bsd', _ctx_2048c, _ctx_2048P)
        _ctx_2048t = _ctx_2048t * jax.lax.rsqrt(jnp.mean(jnp.square(_ctx_2048t)) + 1e-12) * 0.953939
        ctx_2048 = 0.000189249 + 0.0999589 * (_ctx_2048t + 0.3 * jax.random.normal(jax.random.fold_in(_rk, 611), (32, 64, 256), jnp.float32))
        _validS = jnp.arange(64)[None, :] < _lenS[:, None]
        _validS2 = jnp.arange(64)[None, :] < _lenS2[:, None]
        _causal = jnp.tril(jnp.ones((64, 64), dtype=bool))
        mask_Bx1xSxS2_ff0 = jnp.where(jnp.ones((32, 1, 64, 64), dtype=bool), 0.0, -1000000000.0).astype(jnp.float32)
        return (x, ctx_2048, mask_Bx1xSxS2_ff0)
    x, ctx_2048, mask_Bx1xSxS2_ff0 = _rec_inputs()

    def _L0_xattn_setup():
        import jax, jax.numpy as jnp
        import numpy as np
        E, H, L, B = (256, 32, 128, 4)
        S = E // H
        DM, DD = (32, 64)

        def _ln(x, w, b, eps=1e-05):
            m = x.mean(-1, keepdims=True)
            v = ((x - m) ** 2).mean(-1, keepdims=True)
            return (x - m) / jnp.sqrt(v + eps) * w + b

        def _block(x, state, ln1_w, ln1_b, ln2_w, ln2_b, maa_x, maa_w1, maa_w2, maa_stack, time_decay, td_w1, td_w2, u, Wr, Wk, Wv, Wg, Wo, gn_w, gn_b, ffn_maa_k, ffn_maa_r, Wfk, Wfr, Wfv):
            b, l, e = x.shape
            h = u.shape[0]
            s_ = e // h
            xa = _ln(x, ln1_w, ln1_b)
            sx = jnp.concatenate([state[:, 1:2] - xa[:, :1], xa[:, :-1] - xa[:, 1:]], axis=1)
            xxx = jnp.tanh((xa + sx * maa_x) @ maa_w1).reshape(b, l, 5, DM)
            xxx = jnp.einsum('blfd,fde->blfe', xxx, maa_w2)
            xm = xa[:, :, None] + sx[:, :, None] * (maa_stack + xxx)
            xk, xw, xv, xr, xg = (xm[:, :, j] for j in range(5))
            w = jnp.exp(-jnp.exp(time_decay + jnp.tanh(xw @ td_w1) @ td_w2)).reshape(b, l, h, s_)
            r = (xr @ Wr.T).reshape(b, l, h, s_)
            k = (xk @ Wk.T).reshape(b, l, h, s_)
            v = (xv @ Wv.T).reshape(b, l, h, s_)
            g = jax.nn.silu(xg @ Wg.T)
            s0 = state[:, 2:2 + s_].reshape(b, h, s_, s_)

            def step(s, rkvw):
                r_t, k_t, v_t, w_t = rkvw
                a = k_t[..., :, None] * v_t[..., None, :]
                out = jnp.einsum('bhi,bhij->bhj', r_t, u * a + s)
                s = a + w_t[..., :, None] * s
                return (s, out)
            rkvw = tuple((jnp.moveaxis(t, 1, 0) for t in (r, k, v, w)))
            _, out = jax.lax.scan(step, s0, rkvw)
            out = jnp.moveaxis(out, 0, 1).reshape(b, l, e)
            og = out.reshape(b, l, h, s_)
            m = og.mean(-1, keepdims=True)
            va = ((og - m) ** 2).mean(-1, keepdims=True)
            og = ((og - m) / jnp.sqrt(va + 1e-05)).reshape(b, l, e) * gn_w + gn_b
            x1 = x + og * g @ Wo.T
            xc = _ln(x1, ln2_w, ln2_b)
            sx2 = jnp.concatenate([state[:, 0:1] - xc[:, :1], xc[:, :-1] - xc[:, 1:]], axis=1)
            xk2 = xc + sx2 * ffn_maa_k
            xr2 = xc + sx2 * ffn_maa_r
            rr = jax.nn.sigmoid(xr2 @ Wfr.T)
            kk = jnp.square(jax.nn.relu(xk2 @ Wfk.T))
            return x1 + rr * (kk @ Wfv.T)
        key = jax.random.key(seed)
        ks = jax.random.split(key, 24)
        sc = 0.02
        d = {'x': jax.random.normal(ks[0], (B, L, E), jnp.float32), 'state': jax.random.normal(ks[1], (B, 2 + S, E), jnp.float32) * 0.1, 'ln1_w': jnp.ones((E,), jnp.float32), 'ln1_b': jnp.zeros((E,), jnp.float32), 'ln2_w': jnp.ones((E,), jnp.float32), 'ln2_b': jnp.zeros((E,), jnp.float32), 'maa_x': jax.random.normal(ks[2], (E,), jnp.float32) * 0.1, 'maa_w1': jax.random.normal(ks[3], (E, 5 * DM), jnp.float32) * sc, 'maa_w2': jax.random.normal(ks[4], (5, DM, E), jnp.float32) * sc, 'maa_stack': jax.random.normal(ks[5], (1, 5, E), jnp.float32) * 0.1, 'time_decay': jax.random.normal(ks[6], (E,), jnp.float32) * 0.5, 'td_w1': jax.random.normal(ks[7], (E, DD), jnp.float32) * sc, 'td_w2': jax.random.normal(ks[8], (DD, E), jnp.float32) * sc, 'u': jax.random.normal(ks[9], (H, S, 1), jnp.float32) * 0.1, 'Wr': jax.random.normal(ks[10], (E, E), jnp.float32) * sc, 'Wk': jax.random.normal(ks[11], (E, E), jnp.float32) * sc, 'Wv': jax.random.normal(ks[12], (E, E), jnp.float32) * sc, 'Wg': jax.random.normal(ks[13], (E, E), jnp.float32) * sc, 'Wo': jax.random.normal(ks[14], (E, E), jnp.float32) * sc, 'gn_w': jnp.ones((E,), jnp.float32), 'gn_b': jnp.zeros((E,), jnp.float32), 'ffn_maa_k': jax.random.normal(ks[15], (E,), jnp.float32) * 0.1, 'ffn_maa_r': jax.random.normal(ks[16], (E,), jnp.float32) * 0.1, 'Wfk': jax.random.normal(ks[17], (E, E), jnp.float32) * sc, 'Wfr': jax.random.normal(ks[18], (E, E), jnp.float32) * sc, 'Wfv': jax.random.normal(ks[19], (E, E), jnp.float32) * sc}
        return d
    _L0_xattn_all = _L0_xattn_setup()
    _L0_xattn_in = {k: v for k, v in _L0_xattn_all.items() if k in ('ln1_w', 'ln1_b', 'ln2_w', 'ln2_b', 'maa_x', 'maa_w1', 'maa_w2', 'maa_stack', 'time_decay', 'td_w1', 'td_w2', 'u', 'Wr', 'Wk', 'Wv', 'Wg', 'Wo', 'gn_w', 'gn_b', 'ffn_maa_k', 'ffn_maa_r', 'Wfk', 'Wfr', 'Wfv')}
    del _L0_xattn_all

    def _L1_xattn_setup():
        import jax, jax.numpy as jnp
        import numpy as np
        H = 256
        NH = 32
        KVH = 8
        HD = H // NH
        GROUPS = NH // KVH
        EPS = 1e-06
        B, L, S = (4, 128, 128)

        def _gqa_forward(hidden_state, encoder_hidden_state, encoder_attention_mask, Wq, bq, Wk, bk, Wv, bv, Wo, bo, gamma, beta):
            b, l, _ = hidden_state.shape
            s = encoder_hidden_state.shape[1]
            q = hidden_state @ Wq + bq
            k = encoder_hidden_state @ Wk + bk
            v = encoder_hidden_state @ Wv + bv
            q = q.reshape(b, l, KVH, GROUPS, HD).transpose(0, 2, 3, 1, 4)
            k = k.reshape(b, s, KVH, HD).transpose(0, 2, 1, 3)
            v = v.reshape(b, s, KVH, HD).transpose(0, 2, 1, 3)
            scale = 1.0 / jnp.sqrt(jnp.asarray(HD, q.dtype))
            scores = jnp.einsum('bkgld,bksd->bkgls', q, k) * scale
            scores = scores + encoder_attention_mask[:, :, None, :, :]
            attn = jax.nn.softmax(scores, axis=-1)
            out = jnp.einsum('bkgls,bksd->bkgld', attn, v)
            out = out.transpose(0, 3, 1, 2, 4).reshape(b, l, H)
            out = out @ Wo + bo
            x = out + hidden_state
            mu = jnp.mean(x, axis=-1, keepdims=True)
            var = jnp.var(x, axis=-1, keepdims=True)
            return (x - mu) * jax.lax.rsqrt(var + EPS) * gamma + beta
        key = jax.random.key(seed)
        ks = jax.random.split(key, 12)
        sd = 0.02
        return {'hidden_state': jax.random.normal(ks[0], (B, L, H), jnp.float32), 'encoder_hidden_state': jax.random.normal(ks[1], (B, S, H), jnp.float32), 'encoder_attention_mask': jnp.zeros((B, 1, L, S), jnp.float32), 'Wq': jax.random.normal(ks[2], (H, H), jnp.float32) * sd, 'bq': jnp.zeros((H,), jnp.float32), 'Wk': jax.random.normal(ks[3], (H, KVH * HD), jnp.float32) * sd, 'bk': jnp.zeros((KVH * HD,), jnp.float32), 'Wv': jax.random.normal(ks[4], (H, KVH * HD), jnp.float32) * sd, 'bv': jnp.zeros((KVH * HD,), jnp.float32), 'Wo': jax.random.normal(ks[5], (H, H), jnp.float32) * sd, 'bo': jnp.zeros((H,), jnp.float32), 'gamma': jnp.ones((H,), jnp.float32), 'beta': jnp.zeros((H,), jnp.float32)}
    _L1_xattn_all = _L1_xattn_setup()
    _L1_xattn_in = {k: v for k, v in _L1_xattn_all.items() if k in ('Wq', 'bq', 'Wk', 'bk', 'Wv', 'bv', 'Wo', 'bo', 'gamma', 'beta')}
    del _L1_xattn_all
    return {'x': x, 'ctx_2048': ctx_2048, 'mask_Bx1xSxS2_ff0': mask_Bx1xSxS2_ff0, 'L0_xattn_ln1_w': _L0_xattn_in['ln1_w'], 'L0_xattn_ln1_b': _L0_xattn_in['ln1_b'], 'L0_xattn_ln2_w': _L0_xattn_in['ln2_w'], 'L0_xattn_ln2_b': _L0_xattn_in['ln2_b'], 'L0_xattn_maa_x': _L0_xattn_in['maa_x'], 'L0_xattn_maa_w1': _L0_xattn_in['maa_w1'], 'L0_xattn_maa_w2': _L0_xattn_in['maa_w2'], 'L0_xattn_maa_stack': _L0_xattn_in['maa_stack'], 'L0_xattn_time_decay': _L0_xattn_in['time_decay'], 'L0_xattn_td_w1': _L0_xattn_in['td_w1'], 'L0_xattn_td_w2': _L0_xattn_in['td_w2'], 'L0_xattn_u': _L0_xattn_in['u'], 'L0_xattn_Wr': _L0_xattn_in['Wr'], 'L0_xattn_Wk': _L0_xattn_in['Wk'], 'L0_xattn_Wv': _L0_xattn_in['Wv'], 'L0_xattn_Wg': _L0_xattn_in['Wg'], 'L0_xattn_Wo': _L0_xattn_in['Wo'], 'L0_xattn_gn_w': _L0_xattn_in['gn_w'], 'L0_xattn_gn_b': _L0_xattn_in['gn_b'], 'L0_xattn_ffn_maa_k': _L0_xattn_in['ffn_maa_k'], 'L0_xattn_ffn_maa_r': _L0_xattn_in['ffn_maa_r'], 'L0_xattn_Wfk': _L0_xattn_in['Wfk'], 'L0_xattn_Wfr': _L0_xattn_in['Wfr'], 'L0_xattn_Wfv': _L0_xattn_in['Wfv'], 'L1_xattn_Wq': _L1_xattn_in['Wq'], 'L1_xattn_bq': _L1_xattn_in['bq'], 'L1_xattn_Wk': _L1_xattn_in['Wk'], 'L1_xattn_bk': _L1_xattn_in['bk'], 'L1_xattn_Wv': _L1_xattn_in['Wv'], 'L1_xattn_bv': _L1_xattn_in['bv'], 'L1_xattn_Wo': _L1_xattn_in['Wo'], 'L1_xattn_bo': _L1_xattn_in['bo'], 'L1_xattn_gamma': _L1_xattn_in['gamma'], 'L1_xattn_beta': _L1_xattn_in['beta']}

def reference(x, ctx_2048, mask_Bx1xSxS2_ff0, L0_xattn_ln1_w, L0_xattn_ln1_b, L0_xattn_ln2_w, L0_xattn_ln2_b, L0_xattn_maa_x, L0_xattn_maa_w1, L0_xattn_maa_w2, L0_xattn_maa_stack, L0_xattn_time_decay, L0_xattn_td_w1, L0_xattn_td_w2, L0_xattn_u, L0_xattn_Wr, L0_xattn_Wk, L0_xattn_Wv, L0_xattn_Wg, L0_xattn_Wo, L0_xattn_gn_w, L0_xattn_gn_b, L0_xattn_ffn_maa_k, L0_xattn_ffn_maa_r, L0_xattn_Wfk, L0_xattn_Wfr, L0_xattn_Wfv, L1_xattn_Wq, L1_xattn_bq, L1_xattn_Wk, L1_xattn_bk, L1_xattn_Wv, L1_xattn_bv, L1_xattn_Wo, L1_xattn_bo, L1_xattn_gamma, L1_xattn_beta):
    import jax
    import jax.numpy as jnp

    def _L0_xattn_ref(x, state, ln1_w, ln1_b, ln2_w, ln2_b, maa_x, maa_w1, maa_w2, maa_stack, time_decay, td_w1, td_w2, u, Wr, Wk, Wv, Wg, Wo, gn_w, gn_b, ffn_maa_k, ffn_maa_r, Wfk, Wfr, Wfv):
        import jax, jax.numpy as jnp
        import numpy as np
        E, H, L, B = (256, 32, 128, 4)
        S = E // H
        DM, DD = (32, 64)

        def _ln(x, w, b, eps=1e-05):
            m = x.mean(-1, keepdims=True)
            v = ((x - m) ** 2).mean(-1, keepdims=True)
            return (x - m) / jnp.sqrt(v + eps) * w + b

        def _block(x, state, ln1_w, ln1_b, ln2_w, ln2_b, maa_x, maa_w1, maa_w2, maa_stack, time_decay, td_w1, td_w2, u, Wr, Wk, Wv, Wg, Wo, gn_w, gn_b, ffn_maa_k, ffn_maa_r, Wfk, Wfr, Wfv):
            b, l, e = x.shape
            h = u.shape[0]
            s_ = e // h
            xa = _ln(x, ln1_w, ln1_b)
            sx = jnp.concatenate([state[:, 1:2] - xa[:, :1], xa[:, :-1] - xa[:, 1:]], axis=1)
            xxx = jnp.tanh((xa + sx * maa_x) @ maa_w1).reshape(b, l, 5, DM)
            xxx = jnp.einsum('blfd,fde->blfe', xxx, maa_w2)
            xm = xa[:, :, None] + sx[:, :, None] * (maa_stack + xxx)
            xk, xw, xv, xr, xg = (xm[:, :, j] for j in range(5))
            w = jnp.exp(-jnp.exp(time_decay + jnp.tanh(xw @ td_w1) @ td_w2)).reshape(b, l, h, s_)
            r = (xr @ Wr.T).reshape(b, l, h, s_)
            k = (xk @ Wk.T).reshape(b, l, h, s_)
            v = (xv @ Wv.T).reshape(b, l, h, s_)
            g = jax.nn.silu(xg @ Wg.T)
            s0 = state[:, 2:2 + s_].reshape(b, h, s_, s_)

            def step(s, rkvw):
                r_t, k_t, v_t, w_t = rkvw
                a = k_t[..., :, None] * v_t[..., None, :]
                out = jnp.einsum('bhi,bhij->bhj', r_t, u * a + s)
                s = a + w_t[..., :, None] * s
                return (s, out)
            rkvw = tuple((jnp.moveaxis(t, 1, 0) for t in (r, k, v, w)))
            _, out = jax.lax.scan(step, s0, rkvw)
            out = jnp.moveaxis(out, 0, 1).reshape(b, l, e)
            og = out.reshape(b, l, h, s_)
            m = og.mean(-1, keepdims=True)
            va = ((og - m) ** 2).mean(-1, keepdims=True)
            og = ((og - m) / jnp.sqrt(va + 1e-05)).reshape(b, l, e) * gn_w + gn_b
            x1 = x + og * g @ Wo.T
            xc = _ln(x1, ln2_w, ln2_b)
            sx2 = jnp.concatenate([state[:, 0:1] - xc[:, :1], xc[:, :-1] - xc[:, 1:]], axis=1)
            xk2 = xc + sx2 * ffn_maa_k
            xr2 = xc + sx2 * ffn_maa_r
            rr = jax.nn.sigmoid(xr2 @ Wfr.T)
            kk = jnp.square(jax.nn.relu(xk2 @ Wfk.T))
            return x1 + rr * (kk @ Wfv.T)
        return _block(x, state, ln1_w, ln1_b, ln2_w, ln2_b, maa_x, maa_w1, maa_w2, maa_stack, time_decay, td_w1, td_w2, u, Wr, Wk, Wv, Wg, Wo, gn_w, gn_b, ffn_maa_k, ffn_maa_r, Wfk, Wfr, Wfv)

    def _L1_xattn_ref(hidden_state, encoder_hidden_state, encoder_attention_mask, Wq, bq, Wk, bk, Wv, bv, Wo, bo, gamma, beta):
        import jax, jax.numpy as jnp
        import numpy as np
        H = 256
        NH = 32
        KVH = 8
        HD = H // NH
        GROUPS = NH // KVH
        EPS = 1e-06
        B, L, S = (4, 128, 128)

        def _gqa_forward(hidden_state, encoder_hidden_state, encoder_attention_mask, Wq, bq, Wk, bk, Wv, bv, Wo, bo, gamma, beta):
            b, l, _ = hidden_state.shape
            s = encoder_hidden_state.shape[1]
            q = hidden_state @ Wq + bq
            k = encoder_hidden_state @ Wk + bk
            v = encoder_hidden_state @ Wv + bv
            q = q.reshape(b, l, KVH, GROUPS, HD).transpose(0, 2, 3, 1, 4)
            k = k.reshape(b, s, KVH, HD).transpose(0, 2, 1, 3)
            v = v.reshape(b, s, KVH, HD).transpose(0, 2, 1, 3)
            scale = 1.0 / jnp.sqrt(jnp.asarray(HD, q.dtype))
            scores = jnp.einsum('bkgld,bksd->bkgls', q, k) * scale
            scores = scores + encoder_attention_mask[:, :, None, :, :]
            attn = jax.nn.softmax(scores, axis=-1)
            out = jnp.einsum('bkgls,bksd->bkgld', attn, v)
            out = out.transpose(0, 3, 1, 2, 4).reshape(b, l, H)
            out = out @ Wo + bo
            x = out + hidden_state
            mu = jnp.mean(x, axis=-1, keepdims=True)
            var = jnp.var(x, axis=-1, keepdims=True)
            return (x - mu) * jax.lax.rsqrt(var + EPS) * gamma + beta
        return _gqa_forward(hidden_state, encoder_hidden_state, encoder_attention_mask, Wq, bq, Wk, bk, Wv, bv, Wo, bo, gamma, beta)
    x = _L0_xattn_ref(x, ctx_2048, L0_xattn_ln1_w, L0_xattn_ln1_b, L0_xattn_ln2_w, L0_xattn_ln2_b, L0_xattn_maa_x, L0_xattn_maa_w1, L0_xattn_maa_w2, L0_xattn_maa_stack, L0_xattn_time_decay, L0_xattn_td_w1, L0_xattn_td_w2, L0_xattn_u, L0_xattn_Wr, L0_xattn_Wk, L0_xattn_Wv, L0_xattn_Wg, L0_xattn_Wo, L0_xattn_gn_w, L0_xattn_gn_b, L0_xattn_ffn_maa_k, L0_xattn_ffn_maa_r, L0_xattn_Wfk, L0_xattn_Wfr, L0_xattn_Wfv)
    x = _L1_xattn_ref(x, ctx_2048, mask_Bx1xSxS2_ff0, L1_xattn_Wq, L1_xattn_bq, L1_xattn_Wk, L1_xattn_bk, L1_xattn_Wv, L1_xattn_bv, L1_xattn_Wo, L1_xattn_bo, L1_xattn_gamma, L1_xattn_beta)
    return x

_drawn_inputs = setup_inputs


def setup_inputs(seed=0):
    import zlib

    import numpy as np

    out = dict(_drawn_inputs(seed))
    spreads = {'L0_xattn_ln1_w': (1.0, 0.561),
     'L0_xattn_ln1_b': (0.0, 0.565),
     'L0_xattn_ln2_w': (1.0, 0.6),
     'L0_xattn_ln2_b': (0.0, 0.8),
     'L0_xattn_gn_w': (1.0, 0.6),
     'L0_xattn_gn_b': (0.0, 0.8),
     'L1_xattn_bq': (0.0, 0.8),
     'L1_xattn_bk': (0.0, 2.0),
     'L1_xattn_bv': (0.0, 0.694),
     'L1_xattn_bo': (0.0, 0.1),
     'L1_xattn_gamma': (1.0, 0.2),
     'L1_xattn_beta': (0.0, 0.1)}
    factors = {'ctx_2048': 5.738,
     'L0_xattn_maa_x': 8.0,
     'L0_xattn_maa_w1': 6.949,
     'L0_xattn_maa_w2': 6.96,
     'L0_xattn_maa_stack': 2.681,
     'L0_xattn_time_decay': 2.774,
     'L0_xattn_td_w1': 8.0,
     'L0_xattn_td_w2': 8.0,
     'L0_xattn_u': 5.421,
     'L0_xattn_ffn_maa_k': 8.0,
     'L0_xattn_ffn_maa_r': 8.0,
     'L0_xattn_Wfk': 3.004,
     'L0_xattn_Wfr': 8.0,
     'L0_xattn_Wfv': 2.774,
     'L1_xattn_Wq': 8.0,
     'L1_xattn_Wk': 8.0,
     'L1_xattn_Wv': 8.0}
    for name, (base, spread) in spreads.items():
        noise = np.random.default_rng([zlib.crc32(name.encode()), seed]).standard_normal(out[name].shape)
        drawn = base * np.exp(spread * noise) if base else spread * noise
        out[name] = jnp.asarray(drawn.astype(out[name].dtype))
    for name, factor in factors.items():
        out[name] = (out[name] * factor).astype(out[name].dtype)
    return out
```

```python
import concourse.bass as bass
from concourse import mybir
from contextlib import ExitStack

B, L, E, H, S = 32, 64, 256, 32, 8
P = 128
GB = 8
G = B // GB
T = GB * L
NT = T // P
DM, DD = 32, 64
KVH, GR = 8, 4
NST = 16

WEIGHTS = [("w1", 5 * DM), ("td1", DD), ("Wv", E), ("Wk", E), ("Wr", E), ("Wg", E), ("Wo", E), ("Wfk", E),
           ("Wfr", E), ("Wfv", E), ("Q", E), ("K", E), ("V", KVH * S), ("O", E)]
W_AT, W_ALL = {}, 0
for _n, _w in WEIGHTS:
    W_AT[_n] = (W_ALL, _w)
    W_ALL += _w
W_FIRST = W_AT["Wo"][0]
VECS = ["ln1_w", "ln1_b", "ln2_w", "ln2_b", "maa_x", "st0", "st1", "st2", "st3", "st4", "decay", "u",
        "gn_w", "gn_b", "fk", "fr", "bq", "bk"]
VI = {n: i for i, n in enumerate(VECS)}
C_ID, C_R, C_S, C_SUM, C_AVG, C_CEN, NCONST = 0, 1, 9, 17, 18, 19, 20
M_G, M_K, M_X, NMASK = 0, 4, 8, 10
NROW = 3 * E + KVH * S


def xattn_kernel(nc, x, ctxT, s0_in, mask, wpack, w2a, w2b, td2, vecs, consts, masks, rows, out):
    f32 = mybir.dt.float32
    ALU = mybir.AluOpType
    ACT = mybir.ActivationFunctionType
    AX = mybir.AxisListType
    MUL, ADD, SUB, MAX = ALU.mult, ALU.add, ALU.subtract, ALU.max

    es = ExitStack()
    with es:
        def sb(name, shape):
            return es.enter_context(nc.sbuf_tensor(name, shape, f32))

        Wt = sb("Wt", [P, 2, W_ALL])
        w2at = sb("w2at", [P, E])
        w2bt = sb("w2bt", [DM, E])
        td2t = sb("td2t", [DD, E])
        vt = sb("vt", [P, 2, len(VECS)])
        Ct = sb("Ct", [P, NCONST, P])
        mk = sb("mk", [P, NMASK])
        rowt = sb("rowt", [P, NROW])
        qsc = sb("qsc", [P, GR])
        qbi = sb("qbi", [P, 2, GR])
        kbi = sb("kbi", [P, 2, 4])
        bvx = sb("bvx", [P, 2, 4, S])
        gnh = sb("gnh", [P, 2, 2])
        eps5 = sb("eps5", [P, 1])
        mhalf = sb("mhalf", [P, NT])
        marks = sb("marks", [P, 3])
        minus = sb("minus", [P, NT])
        epst = [sb(f"epst{k}", [P, NT]) for k in range(3)]
        xt = sb("xt", [P, NT, E])
        ct = sb("ct", [P, 2, GB, L])
        s0t = sb("s0t", [P, 2, GB, S])
        mt = sb("mt", [P, GB, L])
        stats = [sb(f"stats{k}", [P, NT, 6]) for k in range(3)]
        mv = [sb(f"mv{k}", [P, NT, 2]) for k in range(3)]
        rs = [sb(f"rs{k}", [P, 4, NT]) for k in range(3)]
        xn = sb("xn", [P, NT, E])
        xs = sb("xs", [P, 2, GB, L + 1])
        sx = sb("sx", [P, 2, GB, L])
        xmx = sb("xmx", [P, 2, GB, L])
        h1a = sb("h1a", [P, T])
        h1b = sb("h1b", [DM, T])
        tj = sb("tj", [P, 2, GB, L])
        xm = [sb(f"xm{j}", [P, 2, GB, L]) for j in range(5)]
        hw = sb("hw", [DD, T])
        wS = sb("wS", [P, 2, GB, L])
        vT = sb("vT", [P, 2, GB, L])
        kT = sb("kT", [P, 2, GB, L])
        rT = sb("rT", [P, 2, GB, L])
        thg = sb("thg", [P, 2, T])
        g2 = sb("g2", [P, 2, T])
        uv = sb("uv", [P, 2, T])
        aS = sb("aS", [P, 2, GB, L])
        Sr = sb("Sr", [P, 3, GB, L])
        pr = sb("pr", [P, 3, GB, L])
        oc = sb("oc", [P, 2, T])
        sq = sb("sq", [P, 2, T])
        hid = sb("hid", [P, NT, E])
        hb = sb("hb", [P, NT, E])
        qd = sb("qd", [P, 2, GB, GR, L])
        kd = sb("kd", [P, 2, GB, 4, L])
        Vd = sb("Vd", [P, GB, 4, 2, S + 1])
        nmx = sb("nmx", [P, 3, 8])
        ri2 = sb("ri2", [P, 2, 8])
        On = sb("On", [P, GB, 2, 8, S])
        x3 = sb("x3", [P, NT, E])
        zt = xmx
        ew = xmx
        sc, dx, ex, PTs, OTt = (xm[j] for j in range(5))
        bank = [es.enter_context(nc.psum_tensor(f"bank{i}", [P, 512], f32)) for i in range(8)]

        def b(i, kind=None):
            if kind == "time":
                return bank[i][:, :].rearrange("p (b l) -> p b l", l=L)
            if kind == "token":
                return bank[i][:, :].rearrange("p (t e) -> p t e", e=E)
            return bank[i][:, :]

        def W(n, kh, a=0, w=None):
            at, width = W_AT[n]
            return Wt[:, kh, at + a:at + a + (width if w is None else w)]

        def vec(n, h):
            return vt[:, h, VI[n]:VI[n] + 1]

        def C(i):
            return Ct[:, i, :]

        TD2, VB, KB, RB, GB_ = (1, 2), (3, 4), (5, 6), (7, 0), (1, 2)

        def sem(n):
            return es.enter_context(nc.semaphore(n))

        ld_x, ld_c, ld_s, ld_m, ld_w, ld_w2, ld_cn, ld_v, st_out = map(
            sem, "ld_x ld_c ld_s ld_m ld_w ld_w2 ld_cn ld_v st_out".split())
        d_const, d_set = sem("d_const"), sem("d_set")
        d_bn = [sem(f"d_bn{k}") for k in range(3)]
        d_mv = [sem(f"d_mv{k}") for k in range(3)]
        q_ve = [sem(f"q_ve{k}") for k in range(3)]
        q_rs = [sem(f"q_rs{k}") for k in range(3)]
        q_mr = [sem(f"q_mr{k}") for k in range(3)]
        q_nm = [sem(f"q_nm{k}") for k in range(3)]
        a_xn = [sem(f"a_xn{k}") for k in range(3)]
        p_xT = [sem(f"p_xT{k}") for k in range(2)]
        a_xs = [sem(f"a_xs{k}") for k in range(2)]
        d_row = [sem(f"d_row{k}") for k in range(2)]
        d_sx = [sem(f"d_sx{k}") for k in range(2)]
        (d_xm0, p_h1, a_h1, p_xx, d_tj, q_xm, p_td1, a_hw, p_td2, a_ew, a_w, p_v, a_v, p_k, a_k, p_r, a_r,
         p_g, a_th, d_g2, d_z, p_us, d_uv) = map(sem, (
             "d_xm0 p_h1 a_h1 p_xx d_tj q_xm p_td1 a_hw p_td2 a_ew a_w p_v a_v p_k a_k p_r a_r "
             "p_g a_th d_g2 d_z p_us d_uv").split())
        (p_vr, d_s0, d_a, d_sc, q_pr, p_rd, p_o, a_oc, a_sq) = map(sem, "p_vr d_s0 d_a d_sc q_pr p_rd p_o a_oc a_sq".split())
        (p_var, a_sd, d_ri, d_t1, d_t2, d_og, p_wo, d_x1, d_xkr, p_fk, a_rk, a_kk, p_fr, a_tr, p_fv, d_y1,
         d_hid, q_hb, p_hT, a_hT, p_q, a_qd, p_K, d_kd, p_V, d_V) = map(sem, (
             "p_var a_sd d_ri d_t1 d_t2 d_og p_wo d_x1 d_xkr p_fk a_rk a_kk p_fr a_tr p_fv d_y1 "
             "d_hid q_hb p_hT a_hT p_q a_qd p_K d_kd p_V d_V").split())
        (p_s, d_ms, d_mx, q_dx, a_ex, p_pt, a_pt, p_av, d_ri2, d_on, p_ot, a_ot, p_w1, d_x3, q_fg, q_fb) = map(sem, (
            "p_s d_ms d_mx q_dx a_ex p_pt a_pt p_av d_ri2 d_on p_ot a_ot p_w1 d_x3 q_fg q_fb").split())

        block = es.enter_context(nc.Block())

        @block.sync
        def _(sp):
            def load_x(g):
                sp.dma_start(xt[:, :, :], x[bass.ds(g, 1), :, :, :].rearrange("a p t e -> (a p) t e")).then_inc(ld_x, 16)

            def load_c(g):
                sp.dma_start(ct[:, :, :, :], ctxT[bass.ds(g, 1), :, :, :, :].rearrange("a p h b l -> (a p) h b l")).then_inc(ld_c, 16)

            def load_s(g):
                sp.dma_start(s0t[:, :, :, :], s0_in[bass.ds(g, 1), :, :, :, :].rearrange("a p h b j -> (a p) h b j")).then_inc(ld_s, 16)

            def load_m(g):
                for h in range(2):
                    sp.dma_start(mt[h * L:(h + 1) * L, :, :],
                                 mask[bass.ds(g, 1), :, :, :].rearrange("a l b s -> (a l) b s")).then_inc(ld_m, 16)

            def store(g):
                sp.wait_ge(q_fb, g * NT + NT)
                sp.dma_start(out[bass.ds(g, 1), :, :, :].rearrange("a p t e -> (a p) t e"), x3[:, :, :]).then_inc(st_out, 16)

            load_x(0)
            sp.dma_start(vt[:, :, :], vecs).then_inc(ld_v, 16)
            sp.dma_start(Ct[:, :, :], consts).then_inc(ld_cn, 16)
            load_c(0)
            sp.dma_start(mk[:, :], masks).then_inc(ld_v, 16)
            sp.dma_start(rowt[:, :], rows.rearrange("(a n) -> a n", a=1).to_broadcast([P, NROW])).then_inc(ld_v, 16)
            load_s(0)
            load_m(0)
            with sp.Fori(1, G) as g:
                sp.wait_ge(d_x1, g * 2)
                load_x(g)
                sp.wait_ge(d_s0, g * NST)
                load_s(g)
                sp.wait_ge(p_K, g * 2)
                sp.wait_ge(p_V, g)
                sp.wait_ge(d_row[1], g)
                load_c(g)
                store(g - 1)
                sp.wait_ge(st_out, g * 16)
                sp.wait_ge(d_ms, g * NST)
                load_m(g)
            store(G - 1)
            sp.wait_ge(st_out, G * 16)

        @block.gpsimd
        def _(pool):
            eng = nc.gpsimd

            def rstd(k, g):
                pool.wait_ge(d_mv[k], g * NT + NT)
                if k < 2:
                    pool.wait_ge(a_xn[k], g * NT)
                eng.tensor_tensor(rs[k][:, 0, :], mv[k][:, :, 1], epst[k][:, :], ADD).then_inc(q_ve[k], 1)
                pool.wait_ge(q_ve[k], g + 1)
                eng.tensor_tensor(rs[k][:, 1, :], rs[k][:, 0, :], mhalf[:, :], ALU.pow).then_inc(q_rs[k], 1)
                pool.wait_ge(q_rs[k], g + 1)
                eng.tensor_tensor(rs[k][:, 2, :], rs[k][:, 1, :], mv[k][:, :, 0], MUL).then_inc(q_mr[k], 1)
                pool.wait_ge(q_mr[k], g + 1)
                eng.tensor_tensor(rs[k][:, 3, :], rs[k][:, 2, :], minus[:, :], MUL).then_inc(q_nm[k], 1)

            def mixes(g):
                rstd(0, g)
                pool.wait_ge(p_g, g * 2)
                for n in range(10):
                    j, h = divmod(n, 2)
                    pool.wait_ge(d_tj, g * 10 + n + 1)
                    eng.tensor_tensor(xm[j][:, h, :, :], tj[:, n % 2, :, :], xs[:, h, :, 1:L + 1], ADD).then_inc(q_xm, 1)

            def read_state(g, t):
                pool.wait_ge(d_sc, g * NST + t + 1)
                if t == 0:
                    pool.wait_ge(a_r, g * 2 + 2)
                    pool.wait_ge(p_rd, g * NST)
                if t >= 3:
                    pool.wait_ge(p_rd, g * NST + t - 2)
                eng.tensor_tensor(pr[:, t % 3, :, :], Sr[:, t % 3, :, :], rT[:, t // 8, :, :], MUL).then_inc(q_pr, 1)

            def less_max(g, t):
                pool.wait_ge(d_mx, g * NST + t + 1)
                if t >= 2:
                    pool.wait_ge(a_ex, g * NST + t - 1)
                eng.tensor_tensor(dx[:, t % 2, :, :], sc[:, t % 2, :, :],
                                  nmx[:, t % 3, :].unsqueeze(2).to_broadcast([P, 8, L]), ADD).then_inc(q_dx, 1)

            def residual(g):
                rstd(1, g)
                pool.wait_ge(d_hid, g * 2 + 2)
                pool.wait_ge(d_x3, g * 2)
                eng.tensor_tensor(hb[:, :, :], hid[:, :, :], rowt[:, 0:E].unsqueeze(1).to_broadcast([P, NT, E]), ADD).then_inc(q_hb, 1)

            def finish(g):
                rstd(2, g)
                for t in range(NT):
                    pool.wait_ge(a_xn[2], g * NT + t + 1)
                    eng.tensor_tensor(x3[:, t, :], x3[:, t, :], rowt[:, E:2 * E], MUL).then_inc(q_fg, 1)
                    pool.wait_ge(q_fg, g * NT + t + 1)
                    eng.tensor_tensor(x3[:, t, :], x3[:, t, :], rowt[:, 2 * E:3 * E], ADD).then_inc(q_fb, 1)

            pool.wait_ge(d_const, 7)
            pool.wait_ge(ld_v, 48)
            mixes(0)
            for t in range(NST):
                read_state(0, t)
            residual(0)
            with pool.Fori(1, G) as g:
                mixes(g)
                for t in range(NST):
                    read_state(g, t)
                    less_max(g - 1, t)
                finish(g - 1)
                residual(g)
            for t in range(NST):
                less_max(G - 1, t)
            finish(G - 1)

        @block.scalar
        def _(act):
            eng = nc.scalar
            act.dma_start(Wt[:, :, 0:W_FIRST], wpack[:, :, 0:W_FIRST]).then_inc(ld_w, 16)
            act.dma_start(w2at[:, :], w2a).then_inc(ld_w, 16)
            act.dma_start(w2bt[:, :], w2b).then_inc(ld_w, 16)
            act.dma_start(td2t[:, :], td2).then_inc(ld_w, 16)
            act.dma_start(Wt[:, :, W_FIRST:W_ALL], wpack[:, :, W_FIRST:W_ALL]).then_inc(ld_w2, 16)

            def norm(k, g, dst, src):
                act.wait_ge(q_nm[k], g + 1)
                for t in range(NT):
                    eng.activation(dst[:, t, :], src[:, t, :], ACT.Identity, bias=rs[k][:, 3, t:t + 1],
                                   scale=rs[k][:, 1, t:t + 1]).then_inc(a_xn[k], 1)

            def affine(k, g):
                for h in range(2):
                    act.wait_ge(p_xT[k], g * 2 + h + 1)
                    eng.activation(xs[:, h, :, 1:L + 1], b(h, "time"), ACT.Identity, bias=vec(f"ln{k + 1}_b", h),
                                   scale=vec(f"ln{k + 1}_w", h)).then_inc(a_xs[k], 1)

            def copies(g, made, sig, banks, dst):
                for h in range(2):
                    act.wait_ge(made, g * 2 + h + 1)
                    eng.activation(dst[:, h, :, :], b(banks[h], "time"), ACT.Copy).then_inc(sig, 1)

            def mixes(g):
                act.wait_ge(p_xT[1], g * 2)
                norm(0, g, xn, xt)
                act.wait_ge(d_xkr, g * 4)
                affine(0, g)
                act.wait_ge(p_h1, g * 2 + 1)
                eng.activation(h1a[:, :], b(2), ACT.Tanh).then_inc(a_h1, 1)
                act.wait_ge(p_h1, g * 2 + 2)
                eng.activation(h1b[:, :], bank[3][0:DM, :], ACT.Tanh).then_inc(a_h1, 1)
                act.wait_ge(p_td1, g + 1)
                eng.activation(hw[:, :], bank[0][0:DD, :], ACT.Tanh).then_inc(a_hw, 1)
                act.wait_ge(d_sc, g * NST)
                act.wait_ge(p_us, g * 2)
                act.wait_ge(p_h1, g * 2 + 2)
                for h in range(2):
                    act.wait_ge(p_td2, g * 2 + h + 1)
                    eng.activation(ew[:, h, :, :], b(TD2[h], "time"), ACT.Exp, bias=vec("decay", h)).then_inc(a_ew, 1)
                    act.wait_ge(a_ew, g * 2 + h + 1)
                    eng.activation(wS[:, h, :, 1:L], ew[:, h, :, 0:L - 1], ACT.Exp, scale=-1.0).then_inc(a_w, 1)
                act.wait_ge(p_vr, g * NST)
                act.wait_ge(d_uv, g * 2)
                copies(g, p_v, a_v, VB, vT)
                act.wait_ge(d_a, g * NST)
                copies(g, p_k, a_k, KB, kT)
                act.wait_ge(q_pr, g * NST)
                copies(g, p_r, a_r, RB, rT)
                act.wait_ge(d_y1, g * 2)
                for h in range(2):
                    act.wait_ge(p_g, g * 2 + h + 1)
                    eng.activation(thg[:, h, :], b(GB_[h]), ACT.Tanh, scale=0.5).then_inc(a_th, 1)

            def half_out(g, h):
                act.wait_ge(p_o, g * 2 + h + 1)
                if h == 0:
                    act.wait_ge(p_fv, g * 2)
                eng.activation(oc[:, h, :], b(2), ACT.Copy).then_inc(a_oc, 1)
                eng.activation(sq[:, h, :], b(2), ACT.Square).then_inc(a_sq, 1)

            def exps(g, t):
                act.wait_ge(q_dx, g * NST + t + 1)
                if t >= 2:
                    act.wait_ge(p_pt, g * NST + t - 1)
                eng.activation(ex[:, t % 2, :, :], dx[:, t % 2, :, :], ACT.Exp).then_inc(a_ex, 1)

            def probs(g, t):
                act.wait_ge(p_pt, g * NST + t + 1)
                if t >= 2:
                    act.wait_ge(p_av, g * NST + t - 1)
                eng.activation(PTs[:, t % 2, :, :], b(5 + t % 2, "time"), ACT.Copy).then_inc(a_pt, 1)

            def finish(g):
                for c in range(2):
                    act.wait_ge(p_ot, g * 2 + c + 1)
                    eng.activation(OTt[:, :, 4 * c:4 * c + 4, :],
                                   bank[5 + c][:, :].rearrange("p (b g l) -> p g b l", b=4, g=2), ACT.Copy).then_inc(a_ot, 1)
                norm(2, g, x3, x3)

            def close(g):
                act.wait_ge(d_g2, g * 2 + 2)
                for h in range(2):
                    act.wait_ge(p_var, g * 2 + h + 1)
                    eng.activation(thg[:, h, :], b(h), ACT.Sqrt, bias=eps5[:, :]).then_inc(a_sd, 1)
                act.wait_ge(p_xT[0], g * 2 + 2)
                norm(1, g, xn, hid)
                act.wait_ge(d_tj, g * 10 + 10)
                act.wait_ge(q_xm, g * 10 + 10)
                affine(1, g)
                act.wait_ge(d_t1, g * 2 + 2)
                for h in range(2):
                    act.wait_ge(p_fk, g * 2 + h + 1)
                    eng.activation(sq[:, h, :], b(5 + h), ACT.Relu).then_inc(a_rk, 1)
                    act.wait_ge(a_rk, g * 2 + h + 1)
                    eng.activation(oc[:, h, :], sq[:, h, :], ACT.Square).then_inc(a_kk, 1)
                act.wait_ge(d_ri, g * 2 + 2)
                for c in range(2):
                    act.wait_ge(p_fr, g * 2 + c + 1)
                    eng.activation(thg[:, c, :], b(3 + c), ACT.Tanh, scale=0.5).then_inc(a_tr, 1)
                act.wait_ge(p_wo, g * 2 + 2)
                for h in range(2):
                    act.wait_ge(p_hT, g * 2 + h + 1)
                    eng.activation(g2[:, h, :], b(h), ACT.Copy).then_inc(a_hT, 1)
                act.wait_ge(p_s, g * NST)
                for h in range(2):
                    act.wait_ge(p_q, g * 2 + h + 1)
                    for i in range(GR):
                        eng.activation(qd[:, h, :, i, :], b(5 + h, "time"), ACT.Identity, bias=qbi[:, h, i:i + 1],
                                       scale=qsc[:, i:i + 1]).then_inc(a_qd, 1)

            act.wait_ge(d_const, 7)
            act.wait_ge(d_set, 10)
            act.wait_ge(ld_x, 16)
            mixes(0)
            for t in range(NST):
                if t == 10:
                    half_out(0, 0)
            half_out(0, 1)
            close(0)
            with act.Fori(1, G) as g:
                act.wait_ge(ld_x, g * 16 + 16)
                mixes(g)
                for t in range(NST):
                    if t >= 1:
                        probs(g - 1, t - 1)
                    exps(g - 1, t)
                    if t == 9:
                        half_out(g, 0)
                probs(g - 1, NST - 1)
                half_out(g, 1)
                finish(g - 1)
                close(g)
            for t in range(NST):
                if t >= 1:
                    probs(G - 1, t - 1)
                exps(G - 1, t)
            probs(G - 1, NST - 1)
            finish(G - 1)

        @block.vector
        def _(dve):
            eng = nc.vector

            def moments(k, g, src, ready=None):
                for t in range(NT):
                    if ready is not None and t % 2 == 0:
                        dve.wait_ge(ready, g * 2 + t // 2 + 1)
                    eng.bn_stats(stats[k][:, t, :], src[:, t, :]).then_inc(d_bn[k], 1)
                dve.wait_ge(d_bn[k], g * NT + NT)
                if k < 2:
                    dve.wait_ge(q_nm[k], g)
                eng.tensor_copy(marks[:, k:k + 1], stats[k][:, NT - 1, 0:1])
                for t in range(NT):
                    eng.bn_aggr(mv[k][:, t, :], stats[k][:, t, :]).then_inc(d_mv[k], 1)

            def shifts(k, g):
                for h in range(2):
                    dve.wait_ge(a_xs[k], g * 2 + h + 1)
                    dve.wait_ge(d_row[k], g + 1)
                    eng.tensor_tensor(sx[:, h, :, :], xs[:, h, :, 0:L], xs[:, h, :, 1:L + 1], SUB).then_inc(d_sx[k], 1)

            def mix(k, g, n, h, dst, name, sig):
                dve.wait_ge(d_sx[k], g * 2 + h + 1)
                eng.scalar_tensor_tensor(dst[:, h, :, :], sx[:, h, :, :], vec(name, h), xs[:, h, :, 1:L + 1], MUL, ADD).then_inc(sig, 1)

            def mixes(g):
                dve.wait_ge(ld_x, g * 16 + 16)
                moments(0, g, xt)
                dve.wait_ge(ld_c, g * 16 + 16)
                dve.wait_ge(p_q, g * 2)
                eng.tensor_copy(xs[:, :, :, 0], ct[:, :, :, 1]).then_inc(d_row[0], 1)
                shifts(0, g)
                dve.wait_ge(p_us, g * 2)
                dve.wait_ge(a_w, g * 2)
                for h in range(2):
                    mix(0, g, 0, h, xmx, "maa_x", d_xm0)
                for n in range(10):
                    j, h = divmod(n, 2)
                    dve.wait_ge(p_xx, g * 10 + n + 1)
                    if n >= 2:
                        dve.wait_ge(q_xm, g * 10 + n - 1)
                    eng.scalar_tensor_tensor(tj[:, n % 2, :, :], b(4 + n % 4, "time"), vec(f"st{j}", h), sx[:, h, :, :],
                                             ADD, MUL).then_inc(d_tj, 1)
                dve.wait_ge(a_w, g * 2 + 2)
                for h in range(2):
                    dve.wait_ge(a_r, g * 2 + h + 1)
                    dve.wait_ge(a_k, g * 2 + h + 1)
                    eng.scalar_tensor_tensor(zt[:, h, :, :], rT[:, h, :, :], vec("u", h), kT[:, h, :, :], MUL, MUL).then_inc(d_z, 1)
                dve.wait_ge(p_q, g * 2)
                for h in range(2):
                    dve.wait_ge(a_th, g * 2 + h + 1)
                    eng.scalar_tensor_tensor(g2[:, h, :], thg[:, h, :], 1.0, b(GB_[h]), ADD, MUL).then_inc(d_g2, 1)
                for h in range(2):
                    dve.wait_ge(p_us, g * 2 + h + 1)
                    dve.wait_ge(a_v, g * 2 + h + 1)
                    dve.wait_ge(p_o, g * 2)
                    eng.tensor_tensor(uv[:, h, :], b(3 + h), vT[:, h, :, :].rearrange("p b l -> p (b l)"), MUL).then_inc(d_uv, 1)
                dve.wait_ge(ld_s, g * 16 + 16)

            def recur(g, t):
                h, j = divmod(t, 8)
                n = g * NST + t
                eng.tensor_copy(aS[:, t % 2, :, 0], s0t[:, h, :, j]).then_inc(d_s0, 1)
                dve.wait_ge(p_vr, n + 1)
                eng.tensor_tensor(aS[:, t % 2, :, 1:L], b(t % 2, "time")[:, :, 0:L - 1], kT[:, h, :, 0:L - 1], MUL).then_inc(d_a, 1)
                if t == 0:
                    dve.wait_ge(a_w, g * 2 + 2)
                    dve.wait_ge(q_pr, g * NST)
                if t >= 3:
                    dve.wait_ge(q_pr, n - 2)
                dve.wait_ge(d_a, n + 1)
                dve.wait_ge(d_s0, n + 1)
                fl = "p b l -> p (b l)"
                eng.tensor_tensor_scan(Sr[:, t % 3, :, :].rearrange(fl), wS[:, h, :, :].rearrange(fl),
                                       aS[:, t % 2, :, :].rearrange(fl), 0.0, MUL, ADD).then_inc(d_sc, 1)

            def maxima(g, t):
                n = g * NST + t
                dve.wait_ge(p_s, n + 1)
                if t == 0:
                    dve.wait_ge(ld_m, g * 32 + 32)
                if t >= 2:
                    dve.wait_ge(q_dx, n - 1)
                eng.tensor_tensor(sc[:, t % 2, :, :], b(3 + t % 2, "time"),
                                  mt[:, t // 2, :].unsqueeze(1).to_broadcast([P, 8, L]), ADD).then_inc(d_ms, 1)
                dve.wait_ge(d_ms, n + 1)
                if t >= 3:
                    dve.wait_ge(q_dx, n - 2)
                eng.tensor_reduce(nmx[:, t % 3, :], sc[:, t % 2, :, :], AX.X, MAX, negate=True).then_inc(d_mx, 1)

            def averages(g, t):
                n = g * NST + t
                dve.wait_ge(p_av, n + 1)
                o = bank[7][:, 0:8 * (S + 1)].rearrange("p (k d) -> p k d", d=S + 1)
                eng.reciprocal(ri2[:, t % 2, :], o[:, :, S]).then_inc(d_ri2, 1)
                dve.wait_ge(d_ri2, n + 1)
                eng.tensor_tensor(On[:, t // 2, t % 2, :, :], o[:, :, 0:S],
                                  ri2[:, t % 2, :].unsqueeze(2).to_broadcast([P, 8, S]), MUL).then_inc(d_on, 1)

            def finish(g):
                for c in range(2):
                    dve.wait_ge(p_w1, g * 2 + c + 1)
                    dve.wait_ge(q_hb, g + 1)
                    eng.tensor_tensor(x3[:, 2 * c:2 * c + 2, :], b(3 + c, "token"), hb[:, 2 * c:2 * c + 2, :], ADD).then_inc(d_x3, 1)
                moments(2, g, x3, d_x3)

            def close(g):
                for h in range(2):
                    dve.wait_ge(a_sd, g * 2 + h + 1)
                    eng.reciprocal(sq[:, h, :], thg[:, h, :]).then_inc(d_ri, 1)
                    dve.wait_ge(d_ri, g * 2 + h + 1)
                    dve.wait_ge(a_oc, g * 2 + h + 1)
                    eng.tensor_tensor(oc[:, h, :], oc[:, h, :], sq[:, h, :], MUL).then_inc(d_t1, 1)
                    dve.wait_ge(d_t1, g * 2 + h + 1)
                    eng.tensor_scalar(uv[:, h, :], oc[:, h, :], gnh[:, h, 0:1], gnh[:, h, 1:2], MUL, ADD).then_inc(d_t2, 1)
                    dve.wait_ge(d_t2, g * 2 + h + 1)
                    eng.tensor_tensor(g2[:, h, :], g2[:, h, :], uv[:, h, :], MUL).then_inc(d_og, 1)
                for c in range(2):
                    dve.wait_ge(p_wo, g * 2 + c + 1)
                    eng.tensor_tensor(hid[:, 2 * c:2 * c + 2, :], b((2, 7)[c], "token"), xt[:, 2 * c:2 * c + 2, :], ADD).then_inc(d_x1, 1)
                moments(1, g, hid, d_x1)
                dve.wait_ge(d_tj, g * 10 + 10)
                eng.tensor_copy(xs[:, :, :, 0], ct[:, :, :, 0]).then_inc(d_row[1], 1)
                dve.wait_ge(d_tj, g * 10 + 10)
                shifts(1, g)
                for h in range(2):
                    mix(1, g, 0, h, kT, "fk", d_xkr)
                for h in range(2):
                    mix(1, g, 0, h, rT, "fr", d_xkr)
                for c in range(2):
                    dve.wait_ge(a_tr, g * 2 + c + 1)
                    dve.wait_ge(p_fv, g * 2 + c + 1)
                    v = vT[:, c, :, :].rearrange("p b l -> p (b l)")
                    eng.scalar_tensor_tensor(v, thg[:, c, :], 1.0, b((2, 7)[c]), ADD, MUL).then_inc(d_y1, 1)
                    dve.wait_ge(d_y1, g * 2 + c + 1)
                    dve.wait_ge(a_xn[1], g * NT + 2 * c + 2)
                    eng.scalar_tensor_tensor(hid[:, 2 * c:2 * c + 2, :], v.rearrange("p (t e) -> p t e", e=E), 0.5,
                                             hid[:, 2 * c:2 * c + 2, :], MUL, ADD).then_inc(d_hid, 1)
                for h in range(2):
                    dve.wait_ge(p_K, g * 2 + h + 1)
                    for i in range(4):
                        eng.tensor_scalar(kd[:, h, :, i, :], b(3 + h, "time"), mk[:, M_K + i:M_K + i + 1], kbi[:, h, i:i + 1],
                                          MUL, ADD).then_inc(d_kd, 1)
                dve.wait_ge(p_V, g + 1)
                for i in range(2):
                    eng.scalar_tensor_tensor(
                        Vd[:, :, :, i, 0:S], b(2).rearrange("p (b k x d) -> p b k x d", b=GB, k=4, x=2)[:, :, :, i, :],
                        mk[:, M_X + i:M_X + i + 1], bvx[:, i, :, :].unsqueeze(1).to_broadcast([P, GB, 4, S]),
                        MUL, ADD).then_inc(d_V, 1)

            eng.memset(wS[:, :, :, 0], 0.0).then_inc(d_const, 1)
            eng.memset(eps5[:, :], 1e-5).then_inc(d_const, 1)
            eng.memset(mhalf[:, :], -0.5).then_inc(d_const, 1)
            eng.memset(minus[:, :], -1.0).then_inc(d_const, 1)
            for k in range(3):
                eng.memset(epst[k][:, :], (1e-5, 1e-5, 1e-6)[k]).then_inc(d_const, 1)
            dve.wait_ge(ld_v, 48)
            eng.tensor_scalar(qsc[:, :], mk[:, M_G:M_G + 4], float(S) ** -0.5, None, MUL).then_inc(d_set, 1)
            dve.wait_ge(d_set, 1)
            for h in range(2):
                eng.tensor_scalar(qbi[:, h, :], qsc[:, :], vec("bq", h), None, MUL).then_inc(d_set, 1)
                eng.tensor_scalar(kbi[:, h, :], mk[:, M_K:M_K + 4], vec("bk", h), None, MUL).then_inc(d_set, 1)
                bv = rowt[:, 3 * E:NROW].rearrange("p (k x d) -> p k x d", k=4, x=2)
                eng.tensor_scalar(bvx[:, h, :, :], bv[:, :, h, :], mk[:, M_X + h:M_X + h + 1], None, MUL).then_inc(d_set, 1)
            eng.tensor_scalar(gnh[:, :, :], vt[:, :, VI["gn_w"]:VI["gn_w"] + 2], 0.5, None, MUL).then_inc(d_set, 1)
            for i in range(2):
                eng.tensor_copy(Vd[:, :, :, i, S], mk[:, M_X + i:M_X + i + 1].unsqueeze(1).to_broadcast([P, GB, 4])).then_inc(d_set, 1)
            dve.wait_ge(d_set, 10)
            mixes(0)
            for t in range(NST):
                recur(0, t)
            close(0)
            with dve.Fori(1, G) as g:
                mixes(g)
                for t in range(NST):
                    recur(g, t)
                    maxima(g - 1, t)
                    if t >= 3:
                        averages(g - 1, t - 3)
                for t in range(NST - 3, NST):
                    averages(g - 1, t)
                finish(g - 1)
                close(g)
            for t in range(NST):
                maxima(G - 1, t)
                if t >= 3:
                    averages(G - 1, t - 3)
            for t in range(NST - 3, NST):
                averages(G - 1, t)
            finish(G - 1)

        @block.tensor
        def _(pe):
            mm = nc.tensor.matmul

            def turn(k, g):
                pe.wait_ge(a_xn[k], g * NT + NT)
                for h in range(2):
                    for t in range(NT):
                        i = nc.tensor.transpose(bank[h][:, t * P:(t + 1) * P], xn[:, t, h * P:(h + 1) * P], C(C_ID))
                    i.then_inc(p_xT[k], 1)

            def channels(o, lhs, rhs, sig, m=None):
                for kh in range(2):
                    i = mm(o, lhs(kh), rhs(kh), start=(kh == 0), stop=(kh == 1))
                i.then_inc(sig, 1)

            def full(o, name, src, h, sig):
                channels(b(o, "time"), lambda kh: W(name, kh, h * P, P), lambda kh: src[:, kh, :, :], sig)

            def tokens(o, lhs, name, sig):
                for t in range(2):
                    for kh in range(2):
                        i = mm(b(o, "token")[:, t, :], lhs(t, kh), W(name, kh), start=(kh == 0), stop=(kh == 1))
                i.then_inc(sig, 1)

            def mixes(g):
                pe.wait_ge(a_hT, g * 2)
                turn(0, g)
                pe.wait_ge(d_xm0, g * 2 + 2)
                pe.wait_ge(d_V, g * 2)
                pe.wait_ge(d_kd, g * 8)
                channels(b(2, "time"), lambda kh: W("w1", kh, 0, P), lambda kh: xmx[:, kh, :, :], p_h1)
                channels(bank[3][0:DM, :].rearrange("p (b l) -> p b l", l=L), lambda kh: W("w1", kh, P, DM), lambda kh: xmx[:, kh, :, :], p_h1)
                pe.wait_ge(a_h1, g * 2 + 2)
                pe.wait_ge(a_qd, g * 8)
                pe.wait_ge(d_hid, g * 2)
                for n in range(10):
                    j, h = divmod(n, 2)
                    if n >= 4:
                        pe.wait_ge(d_tj, g * 10 + n - 3)
                    q = slice(DM * j, DM * j + DM)
                    w, a = (w2at[q, h * P:h * P + P], h1a[q, :]) if j < 4 else (w2bt[:, h * P:h * P + P], h1b[:, :])
                    mm(b(4 + n % 4), w, a, start=True, stop=True).then_inc(p_xx, 1)
                pe.wait_ge(q_xm, g * 10 + 4)
                pe.wait_ge(a_xs[0], g * 2 + 2)
                channels(bank[0][0:DD, :].rearrange("p (b l) -> p b l", l=L), lambda kh: W("td1", kh), lambda kh: xm[1][:, kh, :, :], p_td1)
                pe.wait_ge(a_hw, g + 1)
                for h in range(2):
                    mm(b(TD2[h]), td2t[:, h * P:h * P + P], hw[:, :], start=True, stop=True).then_inc(p_td2, 1)
                pe.wait_ge(q_xm, g * 10 + 6)
                pe.wait_ge(d_tj, g * 10 + 10)
                for h in range(2):
                    full(VB[h], "Wv", xm[2], h, p_v)
                for h in range(2):
                    full(KB[h], "Wk", xm[0], h, p_k)
                pe.wait_ge(q_xm, g * 10 + 8)
                for h in range(2):
                    full(RB[h], "Wr", xm[3], h, p_r)
                pe.wait_ge(q_xm, g * 10 + 10)
                pe.wait_ge(a_ew, g * 2 + 2)
                for h in range(2):
                    full(GB_[h], "Wg", xm[4], h, p_g)
                pe.wait_ge(a_v, g * 2 + 2)
                for h in range(2):
                    pe.wait_ge(d_z, g * 2 + h + 1)
                    mm(b(3 + h, "time"), C(C_SUM), zt[:, h, :, :], start=True, stop=True).then_inc(p_us, 1)

            def spread(g, t):
                if t == 0:
                    pe.wait_ge(a_r, g * 2 + 2)
                elif t == 1:
                    pe.wait_ge(d_g2, g * 2 + 2)
                else:
                    pe.wait_ge(d_a, g * NST + t - 1)
                mm(b(t % 2, "time"), C(C_R + t % 8), vT[:, t // 8, :, :], start=True, stop=True).then_inc(p_vr, 1)

            def gather(g, t):
                h, j = divmod(t, 8)
                if j == 0:
                    pe.wait_ge(d_uv, g * 2 + h + 1)
                    if h == 0:
                        pe.wait_ge(d_g2, g * 2 + 2)
                    else:
                        pe.wait_ge(a_sq, g * 2 + 1)
                    mm(b(2), C(C_CEN), uv[:, h, :], start=True, stop=False)
                pe.wait_ge(q_pr, g * NST + t + 1)
                i = mm(b(2, "time"), C(C_S + j), pr[:, t % 3, :, :], start=False, stop=(j == 7))
                i.then_inc(p_rd, 1)
                if j == 7:
                    pe.wait_ge(p_rd, g * NST + t + 1)
                    pe.nop().then_inc(p_o, 1)

            def scores(g, t, last=False):
                bb, h = divmod(t, 2)
                if t == 0 and not last:
                    pe.wait_ge(d_uv, g * 2 + 4)
                if t == 0:
                    pe.wait_ge(a_qd, g * 8 + 8)
                    pe.wait_ge(d_kd, g * 8 + 8)
                if t >= 2:
                    pe.wait_ge(d_ms, g * NST + t - 1)
                for i in range(2):
                    m = mm(bank[3 + t % 2][:, 256 * i:256 * i + 256], qd[:, h, bb, 2 * i:2 * i + 2, :].rearrange("p g l -> p (g l)"),
                           kd[:, h, bb, :, :].rearrange("p k s -> p (k s)"), start=True, stop=True)
                m.then_inc(p_s, 1)

            def turn_probs(g, t):
                pe.wait_ge(a_ex, g * NST + t + 1)
                if t >= 2:
                    pe.wait_ge(a_pt, g * NST + t - 1)
                for i in range(4):
                    m = nc.tensor.transpose(bank[5 + t % 2][:, i * P:(i + 1) * P],
                                            ex[:, t % 2, 2 * i:2 * i + 2, :].rearrange("p k s -> p (k s)"), C(C_ID))
                m.then_inc(p_pt, 1)

            def values(g, t):
                bb, h = divmod(t, 2)
                pe.wait_ge(a_pt, g * NST + t + 1)
                if t == 0:
                    pe.wait_ge(d_V, g * 2 + 2)
                if t >= 1:
                    pe.wait_ge(d_on, g * NST + t)
                for i in range(4):
                    m = mm(bank[7][:, 18 * i:18 * i + 18], PTs[:, t % 2, 2 * i:2 * i + 2, :].rearrange("p k s -> p (k s)"),
                           Vd[:, bb, 2 * h + i % 2, :, :].rearrange("p x d -> p (x d)"), start=True, stop=True)
                m.then_inc(p_av, 1)

            def finish(g):
                for c in range(2):
                    pe.wait_ge(a_pt, g * NST + NST)
                    pe.wait_ge(d_on, g * NST + NST)
                    for i in range(4):
                        m = nc.tensor.transpose(bank[5 + c][:, i * P:(i + 1) * P],
                                                On[:, 4 * c + i, :, :, :].rearrange("p h k d -> p (h k d)"), C(C_ID))
                    m.then_inc(p_ot, 1)
                for c in range(2):
                    pe.wait_ge(a_ot, g * 2 + c + 1)
                    tokens(3 + c, lambda t, gp: OTt[:, gp, 4 * c + 2 * t:4 * c + 2 * t + 2, :].rearrange("p b l -> p (b l)"), "O", p_w1)

            def close(g):
                for h in range(2):
                    pe.wait_ge(a_sq, g * 2 + h + 1)
                    pe.wait_ge(d_a, g * NST + NST)
                    mm(b(h), C(C_AVG), sq[:, h, :], start=True, stop=True).then_inc(p_var, 1)
                pe.wait_ge(ld_w2, 16)
                pe.wait_ge(d_og, g * 2 + 2)
                pe.wait_ge(a_sq, g * 2 + 2)
                for c in range(2):
                    tokens((2, 7)[c], lambda t, kh: g2[:, kh, (2 * c + t) * P:(2 * c + t + 1) * P], "Wo", p_wo)
                pe.wait_ge(a_sd, g * 2 + 2)
                turn(1, g)

                def tok(src):
                    return lambda c: (lambda t, kh: src[:, kh, :, :].rearrange("p b l -> p (b l)")[:, (2 * c + t) * P:(2 * c + t + 1) * P])

                pe.wait_ge(d_xkr, g * 4 + 2)
                for h in range(2):
                    full(5 + h, "Wfk", kT, h, p_fk)
                pe.wait_ge(d_xkr, g * 4 + 4)
                for c in range(2):
                    tokens(3 + c, tok(rT)(c), "Wfr", p_fr)
                pe.wait_ge(a_kk, g * 2 + 2)
                pe.wait_ge(d_x1, g * 2 + 2)
                for c in range(2):
                    tokens((2, 7)[c], lambda t, kh: oc[:, kh, (2 * c + t) * P:(2 * c + t + 1) * P], "Wfv", p_fv)
                pe.wait_ge(a_tr, g * 2 + 2)
                for h in range(2):
                    full(3 + h, "K", ct, h, p_K)
                pe.wait_ge(d_hid, g * 2 + 2)
                pe.wait_ge(a_xs[1], g * 2 + 2)
                for h in range(2):
                    for t in range(NT):
                        i = nc.tensor.transpose(bank[h][:, t * P:(t + 1) * P], hid[:, t, h * P:(h + 1) * P], C(C_ID))
                    i.then_inc(p_hT, 1)
                for bb in range(GB):
                    for xh in range(2):
                        for kh in range(2):
                            i = mm(bank[2][xh * L:(xh + 1) * L, bb * L:(bb + 1) * L], ct[:, kh, bb, :], W("V", kh),
                                   start=(kh == 0), stop=(kh == 1))
                i.then_inc(p_V, 1)
                pe.wait_ge(a_hT, g * 2 + 2)
                for h in range(2):
                    channels(b(5 + h), lambda kh: W("Q", kh, h * P, P), lambda kh: g2[:, kh, :], p_q)

            pe.wait_ge(ld_cn, 16)
            pe.wait_ge(ld_w, 64)
            mixes(0)
            for t in range(NST):
                spread(0, t)
                if t >= 2:
                    gather(0, t - 2)
            gather(0, NST - 2)
            gather(0, NST - 1)
            close(0)
            with pe.Fori(1, G) as g:
                mixes(g)
                for t in range(NST):
                    spread(g, t)
                    scores(g - 1, t)
                    if t >= 1:
                        turn_probs(g - 1, t - 1)
                    if t >= 2:
                        gather(g, t - 2)
                        values(g - 1, t - 2)
                turn_probs(g - 1, NST - 1)
                for t in range(NST - 2, NST):
                    gather(g, t)
                    values(g - 1, t)
                finish(g - 1)
                close(g)
            for t in range(NST):
                scores(G - 1, t, last=True)
                if t >= 1:
                    turn_probs(G - 1, t - 1)
                if t >= 2:
                    values(G - 1, t - 2)
            turn_probs(G - 1, NST - 1)
            for t in range(NST - 2, NST):
                values(G - 1, t)
            finish(G - 1)


def shape_constants():
    import numpy as np
    p = np.arange(P)
    head, sub = p // S, p % S
    same = (head[:, None] == head[None, :])
    c = np.zeros((P, NCONST, P), np.float32)
    c[:, C_ID] = np.eye(P)
    for j in range(S):
        c[:, C_R + j] = same & (sub[:, None] == j)
        c[:, C_S + j] = same * ((sub[None, :] == j) - 1.0 / S)
    c[:, C_SUM] = same
    c[:, C_AVG] = same / float(S)
    c[:, C_CEN] = np.eye(P) - same / float(S)
    m = np.zeros((P, NMASK), np.float32)
    for i in range(4):
        m[:, M_G + i] = (p // S) % GR == i
        m[:, M_K + i] = p // (GR * S) == i
    for i in range(2):
        m[:, M_X + i] = p // L == i
    return c, m


def kernel(**inputs):
    import numpy as np
    import concourse.bacc as bacc
    from concourse import mybir as my
    from concourse.bass_utils import run_bass_kernel_spmd as run

    a = {k: np.asarray(v) for k, v in inputs.items()}
    l0 = {k[len("L0_xattn_"):]: v for k, v in a.items() if k.startswith("L0_xattn_")}
    l1 = {k[len("L1_xattn_"):]: v for k, v in a.items() if k.startswith("L1_xattn_")}

    def halves(w):
        return w.reshape(2, P, -1).transpose(1, 0, 2)

    ctx = a["ctx_2048"]
    wo1 = l1["Wo"].reshape(2, 4, 2, 2, S, E).transpose(3, 0, 2, 1, 4, 5).reshape(E, E)
    wk1 = np.broadcast_to(l1["Wk"].reshape(E, KVH, 1, S), (E, KVH, GR, S)).reshape(E, E)
    bk1 = np.broadcast_to(l1["bk"].reshape(KVH, 1, S), (KVH, GR, S)).reshape(E)
    w = {"w1": l0["maa_w1"], "td1": l0["td_w1"], "Wv": l0["Wv"].T, "Wk": l0["Wk"].T, "Wr": l0["Wr"].T, "Wg": l0["Wg"].T,
         "Wo": l0["Wo"].T, "Wfk": l0["Wfk"].T, "Wfr": l0["Wfr"].T, "Wfv": l0["Wfv"].T, "Q": l1["Wq"], "K": wk1,
         "V": l1["Wv"], "O": wo1}
    v = {"ln1_w": l0["ln1_w"], "ln1_b": l0["ln1_b"], "ln2_w": l0["ln2_w"], "ln2_b": l0["ln2_b"], "maa_x": l0["maa_x"],
         "decay": l0["time_decay"], "u": l0["u"].reshape(E), "gn_w": l0["gn_w"], "gn_b": l0["gn_b"],
         "fk": l0["ffn_maa_k"], "fr": l0["ffn_maa_r"], "bq": l1["bq"], "bk": bk1}
    for j in range(5):
        v[f"st{j}"] = l0["maa_stack"][0, j]
    consts, masks = shape_constants()
    arrays = {
        "x": a["x"].reshape(G, NT, P, E).transpose(0, 2, 1, 3),
        "ctxT": ctx.reshape(G, GB, L, 2, P).transpose(0, 4, 3, 1, 2),
        "s0": ctx[:, 2:2 + S, :].reshape(G, GB, 2, P, S).transpose(0, 3, 2, 1, 4),
        "mask": a["mask_Bx1xSxS2_ff0"].reshape(G, GB, L, L).transpose(0, 2, 1, 3),
        "wpack": np.concatenate([halves(w[n]) for n, _ in WEIGHTS], axis=2),
        "w2a": l0["maa_w2"][:4].reshape(P, E),
        "w2b": l0["maa_w2"][4],
        "td2": l0["td_w2"],
        "vecs": np.stack([v[n].reshape(2, P).T for n in VECS], axis=2),
        "consts": consts,
        "masks": masks,
        "rows": np.concatenate([l1["bo"], l1["gamma"], l1["beta"], l1["bv"]]),
    }
    arrays = {k: np.ascontiguousarray(t) for k, t in arrays.items()}
    nc = bacc.Bacc("TRN2", target_bir_lowering=False, num_devices=1)
    args = [nc.dram_tensor(k, t.shape, my.dt.from_np(t.dtype), kind="ExternalInput").ap() for k, t in arrays.items()]
    out = nc.dram_tensor("out", (G, P, NT, E), my.dt.from_np(np.dtype("float32")), kind="ExternalOutput").ap()
    xattn_kernel(nc, *args, out)
    r = run(nc, [arrays], core_ids=[0])
    return r.results[0]["out"].transpose(0, 2, 1, 3).reshape(B, L, E)
```

```python
import concourse.bass as bass
from concourse import mybir
from contextlib import ExitStack

B, L, E, H, S = 32, 64, 256, 32, 8
P = 128
GB = 8
G = B // GB
T = GB * L
NT = T // P
DM, DD = 32, 64
KVH, GR = 8, 4
NST = 16

WEIGHTS = [("w1", 5 * DM), ("td1", DD), ("Wv", E), ("Wk", E), ("Wr", E), ("Wg", E), ("Wo", E), ("Wfk", E),
           ("Wfr", E), ("Wfv", E), ("Q", E), ("K", E), ("V", KVH * S), ("O", E)]
W_AT, W_ALL = {}, 0
for _n, _w in WEIGHTS:
    W_AT[_n] = (W_ALL, _w)
    W_ALL += _w
W_FIRST = W_AT["Wo"][0]
VECS = ["ln1_w", "ln1_b", "ln2_w", "ln2_b", "maa_x", "st0", "st1", "st2", "st3", "st4", "decay", "u",
        "gn_w", "gn_b", "fk", "fr", "bq", "bk"]
VI = {n: i for i, n in enumerate(VECS)}
C_ID, C_R, C_S, C_SUM, C_CEN, NCONST = 0, 1, 9, 17, 18, 19
C_AVG = NCONST * P
C_SPR = C_AVG + H // 2
C_ALL = C_SPR + 2 * P
M_G, M_K, M_X, NMASK = 0, 4, 8, 10
NSET = 6
NROW = 3 * E + KVH * S


def xattn_kernel(nc, x, ctxT, srows, s0_in, mask, wpack, w2a, w2b, td2, vecs, consts, masks, rows, out):
    f32 = mybir.dt.float32
    ALU = mybir.AluOpType
    ACT = mybir.ActivationFunctionType
    AX = mybir.AxisListType
    MUL, ADD, SUB, MAX = ALU.mult, ALU.add, ALU.subtract, ALU.max

    es = ExitStack()
    with es:
        def sb(name, shape):
            return es.enter_context(nc.sbuf_tensor(name, shape, f32))

        Wt = sb("Wt", [P, 2, W_ALL])
        w2at = sb("w2at", [P, E])
        w2bt = sb("w2bt", [DM, E])
        td2t = sb("td2t", [DD, E])
        vt = sb("vt", [P, 2, len(VECS)])
        Ct = sb("Ct", [P, C_ALL])
        mk = sb("mk", [P, NMASK])
        rowt = sb("rowt", [P, NROW])
        qsc = sb("qsc", [P, GR])
        qbi = sb("qbi", [P, 2, GR])
        kbi = sb("kbi", [P, 2, 4])
        bvx = sb("bvx", [P, 2, 4, S])
        gnh = sb("gnh", [P, 2, 2])
        mhalf = sb("mhalf", [P, NT])
        marks = sb("marks", [P, 3])
        minus = sb("minus", [P, NT])
        epst = [sb(f"epst{k}", [P, NT]) for k in range(3)]
        xt = sb("xt", [P, NT, E])
        ct = sb("ct", [P, 2, GB, L])
        s0t = sb("s0t", [P, 2, GB, S])
        mt = sb("mt", [P, GB, L])
        stats = [sb(f"stats{k}", [P, NT, 6]) for k in range(3)]
        mv = [sb(f"mv{k}", [P, NT, 2]) for k in range(3)]
        rs = [sb(f"rs{k}", [P, 4, NT]) for k in range(3)]
        xn = sb("xn", [P, NT, E])
        srow = sb("srow", [P, 2, G, 2, GB])
        xs = sb("xs", [P, 2, GB, L + 1])
        sx = sb("sx", [P, 2, GB, L])
        xmx = sb("xmx", [P, 2, GB, L])
        h1a = sb("h1a", [P, T])
        h1b = sb("h1b", [DM, T])
        tj = sb("tj", [P, 2, GB, L])
        xm = [sb(f"xm{j}", [P, 2, GB, L]) for j in range(5)]
        hw = h1a[0:DD, :]
        wS = sb("wS", [P, 2, GB, L])
        vT = sb("vT", [P, 2, GB, L])
        kT = sb("kT", [P, 2, GB, L])
        rT = sb("rT", [P, 2, GB, L])
        thg = sb("thg", [P, 2, T])
        g2 = sb("g2", [P, 2, T])
        uv = sb("uv", [P, 2, T])
        aS = sb("aS", [P, 2, GB, L])
        Sr = sb("Sr", [P, 3, GB, L])
        pr = sb("pr", [P, 2, GB, L])
        oc = sb("oc", [P, 2, T])
        sq = sb("sq", [P, 2, T])
        hid = sb("hid", [P, NT, E])
        vs = sb("vs", [P, NT, H])
        vi = sb("vi", [P, NT, H])
        rg = sb("rg", [P, NT, H])
        cb = sb("cb", [P, 2, GB, L])
        xc = sb("xc", [P, 2, GB, L + 1])
        qd = sb("qd", [P, 2, GB, GR, L])
        kd = sb("kd", [P, 2, GB, 4, L])
        Vd = sb("Vd", [P, GB, 4, 2, S + 1])
        nmx = sb("nmx", [P, 3, 8])
        ri2 = sb("ri2", [P, 2, 8])
        On = sb("On", [P, GB, 2, 8, S])
        x3 = sb("x3", [P, NT, E])
        zt = xmx
        ew = xmx
        sc, dx, ex, PTs = (xm[j] for j in range(4))
        bank = [es.enter_context(nc.psum_tensor(f"bank{i}", [P, 512], f32)) for i in range(8)]

        def b(i, kind=None):
            if kind == "time":
                return bank[i][:, :].rearrange("p (b l) -> p b l", l=L)
            if kind == "token":
                return bank[i][:, :].rearrange("p (t e) -> p t e", e=E)
            return bank[i][:, :]

        def W(n, kh, a=0, w=None):
            at, width = W_AT[n]
            return Wt[:, kh, at + a:at + a + (width if w is None else w)]

        def vec(n, h):
            return vt[:, h, VI[n]:VI[n] + 1]

        def C(i):
            return Ct[:, i * P:(i + 1) * P]

        def as_time(t):
            return t.rearrange("p (b l) -> p b l", l=L)

        def as_tokens(t):
            return t[:, :, :, :].rearrange("p h b l -> p (h b l)").rearrange("p (t e) -> p t e", e=E)

        def as_tok2(t):
            return t[:, :, :].rearrange("p h n -> p (h n)").rearrange("p (t e) -> p t e", e=E)

        XA, H1, TD1, TD2, VB, KB, RB, GTB, UB = (0, 1), (2, 3), 2, (3, 0), (1, 2), (3, 0), (1, 2), (3, 0), (1, 2)
        OTB, VAR, W1B, RGB, KEY, SPR, VAL, WOB, XB, FKB, FRB, FVB, HTB, QB = (
            (4, 5), 7, (6, 4), 7, (5, 6), (4, 7), 5, (6, 4), (7, 5), (6, 4), (7, 5), (6, 4), (7, 5), (6, 4))
        VR, SCB, PTB, OB, RO = (0, 1), (2, 3), (4, 5), 6, 7
        XXX = [(j, h) for h in range(2) for j in range(4)] + [(4, 0), (4, 1)]

        def sem(n):
            return es.enter_context(nc.semaphore(n))

        ld_x, ld_c, ld_s, ld_m, ld_w, ld_w2, ld_cn, ld_v, st_out = map(
            sem, "ld_x ld_c ld_s ld_m ld_w ld_w2 ld_cn ld_v st_out".split())
        d_const, d_set = sem("d_const"), sem("d_set")
        d_bn = [sem(f"d_bn{k}") for k in range(3)]
        d_mv = [sem(f"d_mv{k}") for k in range(3)]
        q_ve = [sem(f"q_ve{k}") for k in range(3)]
        q_rs = [sem(f"q_rs{k}") for k in range(3)]
        q_mr = [sem(f"q_mr{k}") for k in range(3)]
        q_nm = [sem(f"q_nm{k}") for k in range(3)]
        a_xn = [sem(f"a_xn{k}") for k in range(3)]
        p_xT = [sem(f"p_xT{k}") for k in range(2)]
        a_xs = [sem(f"a_xs{k}") for k in range(2)]
        d_row = [sem(f"d_row{k}") for k in range(2)]
        d_sx = [sem(f"d_sx{k}") for k in range(2)]
        (d_xm0, p_h1, a_h1, p_xx, d_tj, q_xm, p_td1, a_hw, p_td2, a_ew, a_w, p_v, a_v, p_k, a_k, p_r, a_r,
         p_g, a_th, d_g2, d_z, p_us, d_uv) = map(sem, (
             "d_xm0 p_h1 a_h1 p_xx d_tj q_xm p_td1 a_hw p_td2 a_ew a_w p_v a_v p_k a_k p_r a_r "
             "p_g a_th d_g2 d_z p_us d_uv").split())
        (p_vr, d_s0, d_a, d_sc, q_pr, p_rd, p_o, a_oc, a_sq) = map(sem, "p_vr d_s0 d_a d_sc q_pr p_rd p_o a_oc a_sq".split())
        (p_var, d_vs, d_vi, a_sd, p_rg, a_rg, p_sp, d_t1, d_t2, d_og, p_wo, d_x1, d_mixc, p_fk, a_rk, a_kk, p_fr, a_tr, p_fv, d_y1,
         d_hid, q_hb, p_hT, a_hT, ld_h, p_q, a_qd, p_K, d_kd, p_V, d_V) = map(sem, (
             "p_var d_vs d_vi a_sd p_rg a_rg p_sp d_t1 d_t2 d_og p_wo d_x1 d_mixc p_fk a_rk a_kk p_fr a_tr p_fv d_y1 "
             "d_hid q_hb p_hT a_hT ld_h p_q a_qd p_K d_kd p_V d_V").split())
        (p_s, d_ms, d_mx, q_dx, a_ex, p_pt, a_pt, p_av, d_ri2, d_on, p_ot, a_ot, p_w1, d_x3, q_fg, q_fb) = map(sem, (
            "p_s d_ms d_mx q_dx a_ex p_pt a_pt p_av d_ri2 d_on p_ot a_ot p_w1 d_x3 q_fg q_fb").split())

        block = es.enter_context(nc.Block())

        @block.sync
        def _(sp):
            def load_x(g):
                sp.dma_start(xt[:, :, :], x[bass.ds(g, 1), :, :, :].rearrange("a p t e -> (a p) t e")).then_inc(ld_x, 16)

            def load_c(g):
                sp.dma_start(ct[:, :, :, :], ctxT[bass.ds(g, 1), :, :, :, :].rearrange("a p h b l -> (a p) h b l")).then_inc(ld_c, 16)

            def load_s(g):
                sp.dma_start(s0t[:, :, :, :], s0_in[bass.ds(g, 1), :, :, :, :].rearrange("a p h b j -> (a p) h b j")).then_inc(ld_s, 16)

            def load_m(g):
                for h in range(2):
                    sp.dma_start(mt[h * L:(h + 1) * L, :, :],
                                 mask[bass.ds(g, 1), :, :, :].rearrange("a l b s -> (a l) b s")).then_inc(ld_m, 16)

            def store(g):
                sp.wait_ge(q_fb, g * NT + NT)
                sp.dma_start(out[bass.ds(g, 1), :, :, :].rearrange("a p t e -> (a p) t e"), x3[:, :, :]).then_inc(st_out, 16)

            def load_h(g):
                sp.dma_start(hid[:, :, :], x[bass.ds(g, 1), :, :, :].rearrange("a p t e -> (a p) t e")).then_inc(ld_h, 16)

            load_x(0)
            sp.dma_start(vt[:, :, :], vecs).then_inc(ld_v, 16)
            sp.dma_start(srow[:, :, :, :, :], srows).then_inc(ld_v, 16)
            sp.dma_start(Ct[:, :], consts).then_inc(ld_cn, 16)
            sp.dma_start(mk[:, :], masks).then_inc(ld_v, 16)
            sp.dma_start(rowt[:, :], rows.rearrange("(a n) -> a n", a=1).to_broadcast([P, NROW])).then_inc(ld_v, 16)
            load_s(0)
            load_c(0)
            load_m(0)
            load_h(0)
            sp.wait_ge(a_xn[0], NT)
            load_x(1)
            sp.wait_ge(d_s0, NST)
            load_s(1)
            sp.wait_ge(p_K, 2)
            sp.wait_ge(p_V, 1)
            load_c(1)
            with sp.Fori(2, G) as g:
                sp.wait_ge(a_xn[0], g * NT)
                load_x(g)
                sp.wait_ge(d_s0, g * NST)
                load_s(g)
                sp.wait_ge(d_ms, (g - 1) * NST)
                load_m(g - 1)
                sp.wait_ge(d_x3, (g - 1) * 2)
                load_h(g - 1)
                store(g - 2)
                sp.wait_ge(p_K, g * 2)
                sp.wait_ge(p_V, g)
                sp.wait_ge(st_out, (g - 1) * 16)
                load_c(g)
            sp.wait_ge(d_ms, (G - 1) * NST)
            load_m(G - 1)
            sp.wait_ge(d_x3, (G - 1) * 2)
            load_h(G - 1)
            store(G - 2)
            store(G - 1)
            sp.wait_ge(st_out, G * 16)

        @block.gpsimd
        def _(pool):
            eng = nc.gpsimd

            def rstd(k, g):
                pool.wait_ge(d_mv[k], g * NT + NT)
                if k < 2:
                    pool.wait_ge(a_xn[k], g * NT)
                eng.tensor_tensor(rs[k][:, 0, :], mv[k][:, :, 1], epst[k][:, :], ADD).then_inc(q_ve[k], 1)
                pool.wait_ge(q_ve[k], g + 1)
                eng.tensor_tensor(rs[k][:, 1, :], rs[k][:, 0, :], mhalf[:, :], ALU.pow).then_inc(q_rs[k], 1)
                pool.wait_ge(q_rs[k], g + 1)
                eng.tensor_tensor(rs[k][:, 2, :], rs[k][:, 1, :], mv[k][:, :, 0], MUL).then_inc(q_mr[k], 1)
                pool.wait_ge(q_mr[k], g + 1)
                eng.tensor_tensor(rs[k][:, 3, :], rs[k][:, 2, :], minus[:, :], MUL).then_inc(q_nm[k], 1)

            def add_mixes(g, first, end):
                for n in range(first, end):
                    j, h = XXX[n]
                    pool.wait_ge(d_tj, g * 10 + n + 1)
                    if n == 0:
                        pool.wait_ge(p_g, g * 2)
                    eng.tensor_tensor(xm[j][:, h, :, :], tj[:, n % 2, :, :], xs[:, h, :, 1:L + 1], ADD).then_inc(q_xm, 1)

            def read_state(g, t):
                pool.wait_ge(d_sc, g * NST + t + 1)
                if t == 0:
                    pool.wait_ge(a_r, g * 2 + 2)
                    pool.wait_ge(p_rd, g * NST)
                if t >= 2:
                    pool.wait_ge(p_rd, g * NST + t - 1)
                eng.tensor_tensor(pr[:, t % 2, :, :], Sr[:, t % 3, :, :], rT[:, t // 8, :, :], MUL).then_inc(q_pr, 1)

            def less_max(g, t):
                pool.wait_ge(d_mx, g * NST + t + 1)
                if t >= 2:
                    pool.wait_ge(a_ex, g * NST + t - 1)
                eng.tensor_tensor(dx[:, t % 2, :, :], sc[:, t % 2, :, :],
                                  nmx[:, t % 3, :].unsqueeze(2).to_broadcast([P, 8, L]), ADD).then_inc(q_dx, 1)

            def residual(g):
                pool.wait_ge(d_hid, g * 2 + 2)
                pool.wait_ge(p_hT, g * 2 + 2)
                eng.tensor_tensor(hid[:, :, :], hid[:, :, :], rowt[:, 0:E].unsqueeze(1).to_broadcast([P, NT, E]), ADD).then_inc(q_hb, 1)

            def finish(g):
                for t in range(NT):
                    pool.wait_ge(a_xn[2], g * NT + t + 1)
                    eng.tensor_tensor(x3[:, t, :], x3[:, t, :], rowt[:, E:2 * E], MUL).then_inc(q_fg, 1)
                    pool.wait_ge(q_fg, g * NT + t + 1)
                    eng.tensor_tensor(x3[:, t, :], x3[:, t, :], rowt[:, 2 * E:3 * E], ADD).then_inc(q_fb, 1)

            def part_one(a, c, f):
                if a is not None:
                    rstd(0, a)
                if f is not None:
                    rstd(2, f)
                if a is not None:
                    add_mixes(a, 0, 6)
                if c is not None:
                    rstd(1, c)
                if a is not None:
                    add_mixes(a, 6, 10)
                if f is not None:
                    finish(f)
                if c is not None:
                    residual(c)

            def part_two(r, a):
                for t in range(NST):
                    if r is not None:
                        read_state(r, t)
                    if a is not None:
                        less_max(a, t)

            pool.wait_ge(d_const, NSET)
            pool.wait_ge(ld_v, 64)
            part_one(0, None, None)
            part_two(0, None)
            part_one(1, 0, None)
            part_two(1, 0)
            with pool.Fori(2, G) as g:
                part_one(g, g - 1, g - 2)
                part_two(g, g - 1)
            part_one(None, G - 1, G - 2)
            part_two(None, G - 1)
            rstd(2, G - 1)
            finish(G - 1)

        @block.scalar
        def _(act):
            eng = nc.scalar
            act.dma_start(Wt[:, :, 0:W_FIRST], wpack[:, :, 0:W_FIRST]).then_inc(ld_w, 16)
            act.dma_start(w2at[:, :], w2a).then_inc(ld_w, 16)
            act.dma_start(w2bt[:, :], w2b).then_inc(ld_w, 16)
            act.dma_start(td2t[:, :], td2).then_inc(ld_w, 16)
            act.dma_start(Wt[:, :, W_FIRST:W_ALL], wpack[:, :, W_FIRST:W_ALL]).then_inc(ld_w2, 16)

            def norm(k, g, dst, src):
                act.wait_ge(q_nm[k], g + 1)
                for t in range(NT):
                    eng.activation(dst[:, t, :], src[:, t, :], ACT.Identity, bias=rs[k][:, 3, t:t + 1],
                                   scale=rs[k][:, 1, t:t + 1]).then_inc(a_xn[k], 1)

            def affine(k, g, dst, banks):
                for h in range(2):
                    act.wait_ge(p_xT[k], g * 2 + h + 1)
                    eng.activation(dst[:, h, :, 1:L + 1], b(banks[h], "time"), ACT.Identity, bias=vec(f"ln{k + 1}_b", h),
                                   scale=vec(f"ln{k + 1}_w", h)).then_inc(a_xs[k], 1)

            def copies(g, made, sig, banks, dst):
                for h in range(2):
                    act.wait_ge(made, g * 2 + h + 1)
                    eng.activation(dst[:, h, :, :], b(banks[h], "time"), ACT.Copy).then_inc(sig, 1)

            def half_out(g, h):
                act.wait_ge(p_o, g * 2 + h + 1)
                if h == 0:
                    act.wait_ge(p_fv, g * 2)
                eng.activation(oc[:, h, :], b(RO), ACT.Copy).then_inc(a_oc, 1)
                eng.activation(sq[:, h, :], b(RO), ACT.Square).then_inc(a_sq, 1)

            def exps(g, t):
                act.wait_ge(q_dx, g * NST + t + 1)
                if t >= 2:
                    act.wait_ge(p_pt, g * NST + t - 1)
                eng.activation(ex[:, t % 2, :, :], dx[:, t % 2, :, :], ACT.Exp).then_inc(a_ex, 1)

            def probs(g, t):
                act.wait_ge(p_pt, g * NST + t + 1)
                if t >= 2:
                    act.wait_ge(p_av, g * NST + t - 1)
                eng.activation(PTs[:, t % 2, :, :], b(PTB[t % 2], "time"), ACT.Copy).then_inc(a_pt, 1)

            def turned(f):
                for c in range(2):
                    act.wait_ge(p_ot, f * 2 + c + 1)
                    eng.activation(cb[:, :, 4 * c:4 * c + 4, :],
                                   bank[OTB[c]][:, :].rearrange("p (b g l) -> p g b l", b=4, g=2), ACT.Copy).then_inc(a_ot, 1)

            def part_one(a, c, f):
                if c is not None:
                    half_out(c, 1)
                if f is not None:
                    act.wait_ge(p_q, (f + 1) * 2)
                    turned(f)
                if a is not None:
                    act.wait_ge(ld_x, a * 16 + 16)
                    act.wait_ge(p_xT[0], a * 2)
                    norm(0, a, xn, xt)
                if c is not None:
                    act.wait_ge(d_vi, c + 1)
                    act.wait_ge(p_rg, c)
                    eng.activation(rg[:, :, :], vi[:, :, :], ACT.Sqrt).then_inc(a_sd, 1)
                if a is not None:
                    act.wait_ge(d_xm0, a * 2)
                    act.wait_ge(q_xm, a * 10)
                    affine(0, a, xs, XA)
                if c is not None:
                    act.wait_ge(p_rg, c + 1)
                    if f is not None:
                        act.wait_ge(p_w1, f * 2 + 2)
                    eng.activation(cb[0:H, 0, :, :], bank[RGB][0:H, :].rearrange("p (b l) -> p b l", l=L), ACT.Copy).then_inc(a_rg, 1)
                if a is not None:
                    act.wait_ge(p_h1, a * 2 + 1)
                    act.wait_ge(p_td2, a * 2)
                    eng.activation(h1a[:, :], b(H1[0]), ACT.Tanh).then_inc(a_h1, 1)
                    act.wait_ge(p_h1, a * 2 + 2)
                    eng.activation(h1b[:, :], bank[H1[1]][0:DM, :], ACT.Tanh).then_inc(a_h1, 1)
                if f is not None:
                    norm(2, f, x3, x3)
                if c is not None:
                    act.wait_ge(d_og, c * 2 + 2)
                    norm(1, c, as_tok2(oc), hid)
                if a is not None:
                    act.wait_ge(p_td1, a + 1)
                    act.wait_ge(p_xx, a * 10 + 8)
                    eng.activation(hw, bank[TD1][0:DD, :], ACT.Tanh).then_inc(a_hw, 1)
                    act.wait_ge(d_sc, a * NST)
                    for h in range(2):
                        act.wait_ge(p_td2, a * 2 + h + 1)
                        eng.activation(ew[:, h, :, :], b(TD2[h], "time"), ACT.Exp, bias=vec("decay", h)).then_inc(a_ew, 1)
                        act.wait_ge(a_ew, a * 2 + h + 1)
                        eng.activation(wS[:, h, :, 1:L], ew[:, h, :, 0:L - 1], ACT.Exp, scale=-1.0).then_inc(a_w, 1)
                if c is not None:
                    affine(1, c, xc, XB)
                if a is not None:
                    act.wait_ge(p_vr, a * NST)
                    act.wait_ge(d_uv, a * 2)
                    copies(a, p_v, a_v, VB, vT)
                if c is not None:
                    act.wait_ge(d_mixc, c * 4 + 4)
                    for h in range(2):
                        act.wait_ge(p_fk, c * 2 + h + 1)
                        eng.activation(cb[:, h, :, :], b(FKB[h], "time"), ACT.Relu).then_inc(a_rk, 1)
                        act.wait_ge(a_rk, c * 2 + h + 1)
                        eng.activation(cb[:, h, :, :], cb[:, h, :, :], ACT.Square).then_inc(a_kk, 1)
                if a is not None:
                    act.wait_ge(d_a, a * NST)
                    act.wait_ge(d_z, a * 2)
                    copies(a, p_k, a_k, KB, kT)
                if c is not None:
                    for i in range(2):
                        act.wait_ge(p_fr, c * 2 + i + 1)
                        eng.activation(oc[:, i, :], b(FRB[i]), ACT.Tanh, scale=0.5).then_inc(a_tr, 1)
                if a is not None:
                    act.wait_ge(q_pr, a * NST)
                    copies(a, p_r, a_r, RB, rT)
                    act.wait_ge(d_g2, a * 2)
                    for h in range(2):
                        act.wait_ge(p_g, a * 2 + h + 1)
                        eng.activation(thg[:, h, :], b(GTB[h]), ACT.Tanh, scale=0.5).then_inc(a_th, 1)
                if c is not None:
                    act.wait_ge(p_fv, c * 2 + 2)
                    for h in range(2):
                        act.wait_ge(p_hT, c * 2 + h + 1)
                        eng.activation(cb[:, h, :, :], b(HTB[h], "time"), ACT.Copy).then_inc(a_hT, 1)
                    act.wait_ge(p_s, c * NST)
                    for h in range(2):
                        act.wait_ge(p_q, c * 2 + h + 1)
                        for i in range(GR):
                            eng.activation(qd[:, h, :, i, :], b(QB[h], "time"), ACT.Identity, bias=qbi[:, h, i:i + 1],
                                           scale=qsc[:, i:i + 1]).then_inc(a_qd, 1)

            def part_two(r, a):
                for t in range(NST):
                    if a is not None:
                        if t >= 2:
                            probs(a, t - 2)
                        exps(a, t)
                    if r is not None and t == 9:
                        half_out(r, 0)
                if a is not None:
                    for t in range(NST - 2, NST):
                        probs(a, t)

            act.wait_ge(d_const, NSET)
            act.wait_ge(d_set, 10)
            part_one(0, None, None)
            part_two(0, None)
            part_one(1, 0, None)
            part_two(1, 0)
            with act.Fori(2, G) as g:
                part_one(g, g - 1, g - 2)
                part_two(g, g - 1)
            part_one(None, G - 1, G - 2)
            part_two(None, G - 1)
            act.wait_ge(p_q, G * 2)
            turned(G - 1)
            norm(2, G - 1, x3, x3)

        @block.vector
        def _(dve):
            eng = nc.vector

            def moments(k, g, src, ready=None):
                for t in range(NT):
                    if ready is not None and t % 2 == 0:
                        dve.wait_ge(ready, g * 2 + t // 2 + 1)
                    eng.bn_stats(stats[k][:, t, :], src[:, t, :]).then_inc(d_bn[k], 1)
                dve.wait_ge(d_bn[k], g * NT + NT)
                if k < 2:
                    dve.wait_ge(q_nm[k], g)
                eng.tensor_copy(marks[:, k:k + 1], stats[k][:, NT - 1, 0:1])
                for t in range(NT):
                    eng.bn_aggr(mv[k][:, t, :], stats[k][:, t, :]).then_inc(d_mv[k], 1)

            def shifts(k, g, dst, src, row):
                eng.tensor_copy(src[:, :, :, 0], srow[:, row, bass.ds(g, 1), :, :].rearrange("p a h b -> p (a h) b")).then_inc(d_row[k], 1)
                for h in range(2):
                    dve.wait_ge(a_xs[k], g * 2 + h + 1)
                    dve.wait_ge(d_row[k], g + 1)
                    eng.tensor_tensor(dst[:, h, :, :], src[:, h, :, 0:L], src[:, h, :, 1:L + 1], SUB).then_inc(d_sx[k], 1)

            def mix(k, g, h, dst, shifted, src, name, sig):
                dve.wait_ge(d_sx[k], g * 2 + h + 1)
                eng.scalar_tensor_tensor(dst, shifted[:, h, :, :], vec(name, h), src[:, h, :, 1:L + 1], MUL, ADD).then_inc(sig, 1)

            def scaled_shifts(g, first, end):
                for n in range(first, end):
                    j, h = XXX[n]
                    dve.wait_ge(p_xx, g * 10 + n + 1)
                    if n >= 2:
                        dve.wait_ge(q_xm, g * 10 + n - 1)
                    eng.scalar_tensor_tensor(tj[:, n % 2, :, :], b(n % 4, "time"), vec(f"st{j}", h), sx[:, h, :, :],
                                             ADD, MUL).then_inc(d_tj, 1)

            def recur(g, t):
                h, j = divmod(t, 8)
                n = g * NST + t
                eng.tensor_copy(aS[:, t % 2, :, 0], s0t[:, h, :, j]).then_inc(d_s0, 1)
                dve.wait_ge(p_vr, n + 1)
                eng.tensor_tensor(aS[:, t % 2, :, 1:L], b(t % 2, "time")[:, :, 0:L - 1], kT[:, h, :, 0:L - 1], MUL).then_inc(d_a, 1)
                if t == 0:
                    dve.wait_ge(a_w, g * 2 + 2)
                    dve.wait_ge(q_pr, g * NST)
                if t >= 3:
                    dve.wait_ge(q_pr, n - 2)
                dve.wait_ge(d_a, n + 1)
                dve.wait_ge(d_s0, n + 1)
                fl = "p b l -> p (b l)"
                eng.tensor_tensor_scan(Sr[:, t % 3, :, :].rearrange(fl), wS[:, h, :, :].rearrange(fl),
                                       aS[:, t % 2, :, :].rearrange(fl), 0.0, MUL, ADD).then_inc(d_sc, 1)

            def maxima(g, t):
                n = g * NST + t
                dve.wait_ge(p_s, n + 1)
                if t == 0:
                    dve.wait_ge(ld_m, g * 32 + 32)
                if t >= 2:
                    dve.wait_ge(q_dx, n - 1)
                eng.tensor_tensor(sc[:, t % 2, :, :], b(SCB[t % 2], "time"),
                                  mt[:, t // 2, :].unsqueeze(1).to_broadcast([P, 8, L]), ADD).then_inc(d_ms, 1)
                dve.wait_ge(d_ms, n + 1)
                if t >= 3:
                    dve.wait_ge(q_dx, n - 2)
                eng.tensor_reduce(nmx[:, t % 3, :], sc[:, t % 2, :, :], AX.X, MAX, negate=True).then_inc(d_mx, 1)

            def averages(g, t):
                n = g * NST + t
                dve.wait_ge(p_av, n + 1)
                o = bank[OB][:, 0:8 * (S + 1)].rearrange("p (k d) -> p k d", d=S + 1)
                eng.reciprocal(ri2[:, t % 2, :], o[:, :, S]).then_inc(d_ri2, 1)
                dve.wait_ge(d_ri2, n + 1)
                eng.tensor_tensor(On[:, t // 2, t % 2, :, :], o[:, :, 0:S],
                                  ri2[:, t % 2, :].unsqueeze(2).to_broadcast([P, 8, S]), MUL).then_inc(d_on, 1)

            def finish(g):
                dve.wait_ge(ld_c, min_c(g))
                for c in range(2):
                    dve.wait_ge(p_w1, g * 2 + c + 1)
                    dve.wait_ge(q_hb, g + 1)
                    eng.tensor_tensor(x3[:, 2 * c:2 * c + 2, :], b(W1B[c], "token"), hid[:, 2 * c:2 * c + 2, :], ADD).then_inc(d_x3, 1)
                moments(2, g, x3, d_x3)

            def min_c(g):
                return G * 16 if isinstance(g, int) else (g + 2) * 16

            def part_one(a, c, f):
                if c is not None:
                    dve.wait_ge(p_var, c + 1)
                    eng.tensor_scalar(vs[:, :, :], bank[VAR][:, 0:NT * H].rearrange("p (t k) -> p t k", k=H), 1e-5, None, ADD).then_inc(d_vs, 1)
                    dve.wait_ge(d_vs, c + 1)
                    dve.wait_ge(a_sd, c)
                    eng.reciprocal(vi[:, :, :], vs[:, :, :]).then_inc(d_vi, 1)
                if a is not None:
                    dve.wait_ge(ld_x, a * 16 + 16)
                    moments(0, a, xt)
                    shifts(0, a, sx, xs, 1)
                    dve.wait_ge(p_us, a * 2)
                    dve.wait_ge(a_w, a * 2)
                    for h in range(2):
                        mix(0, a, h, xmx[:, h, :, :], sx, xs, "maa_x", d_xm0)
                if f is not None:
                    finish(f)
                if c is not None:
                    dve.wait_ge(p_s, c * NST)
                    for h in range(2):
                        dve.wait_ge(p_K, c * 2 + h + 1)
                        for i in range(4):
                            eng.tensor_scalar(kd[:, h, :, i, :], b(KEY[h], "time"), mk[:, M_K + i:M_K + i + 1], kbi[:, h, i:i + 1],
                                              MUL, ADD).then_inc(d_kd, 1)
                    for h in range(2):
                        dve.wait_ge(p_sp, c * 2 + h + 1)
                        dve.wait_ge(a_oc, c * 2 + h + 1)
                        eng.tensor_tensor(oc[:, h, :], oc[:, h, :], b(SPR[h]), MUL).then_inc(d_t1, 1)
                        dve.wait_ge(d_t1, c * 2 + h + 1)
                        eng.tensor_scalar(oc[:, h, :], oc[:, h, :], gnh[:, h, 0:1], gnh[:, h, 1:2], MUL, ADD).then_inc(d_t2, 1)
                        dve.wait_ge(d_t2, c * 2 + h + 1)
                        eng.tensor_tensor(sq[:, h, :], g2[:, h, :], oc[:, h, :], MUL).then_inc(d_og, 1)
                    dve.wait_ge(p_V, c + 1)
                    for i in range(2):
                        eng.scalar_tensor_tensor(
                            Vd[:, :, :, i, 0:S], b(VAL).rearrange("p (b k x d) -> p b k x d", b=GB, k=4, x=2)[:, :, :, i, :],
                            mk[:, M_X + i:M_X + i + 1], bvx[:, i, :, :].unsqueeze(1).to_broadcast([P, GB, 4, S]),
                            MUL, ADD).then_inc(d_V, 1)
                if a is not None:
                    scaled_shifts(a, 0, 6)
                if c is not None:
                    dve.wait_ge(ld_h, c * 16 + 16)
                    for i in range(2):
                        dve.wait_ge(p_wo, c * 2 + i + 1)
                        eng.tensor_tensor(hid[:, 2 * i:2 * i + 2, :], b(WOB[i], "token"), hid[:, 2 * i:2 * i + 2, :], ADD).then_inc(d_x1, 1)
                    moments(1, c, hid, d_x1)
                if a is not None:
                    scaled_shifts(a, 6, 10)
                if c is not None:
                    shifts(1, c, cb, xc, 0)
                    for h in range(2):
                        mix(1, c, h, oc[:, h, :].rearrange("p (b l) -> p b l", l=L), cb, xc, "fk", d_mixc)
                    for h in range(2):
                        mix(1, c, h, sq[:, h, :].rearrange("p (b l) -> p b l", l=L), cb, xc, "fr", d_mixc)
                if a is not None:
                    dve.wait_ge(a_w, a * 2 + 2)
                    for h in range(2):
                        dve.wait_ge(a_r, a * 2 + h + 1)
                        dve.wait_ge(a_k, a * 2 + h + 1)
                        eng.scalar_tensor_tensor(zt[:, h, :, :], rT[:, h, :, :], vec("u", h), kT[:, h, :, :], MUL, MUL).then_inc(d_z, 1)
                if c is not None:
                    for i in range(2):
                        dve.wait_ge(a_tr, c * 2 + i + 1)
                        dve.wait_ge(p_fv, c * 2 + i + 1)
                        eng.scalar_tensor_tensor(sq[:, i, :], oc[:, i, :], 1.0, b(FVB[i]), ADD, MUL).then_inc(d_y1, 1)
                        dve.wait_ge(d_y1, c * 2 + i + 1)
                        dve.wait_ge(a_xn[1], c * NT + 2 * i + 2)
                        eng.scalar_tensor_tensor(hid[:, 2 * i:2 * i + 2, :], sq[:, i, :].rearrange("p (t e) -> p t e", e=E), 0.5,
                                                 hid[:, 2 * i:2 * i + 2, :], MUL, ADD).then_inc(d_hid, 1)
                if a is not None:
                    for h in range(2):
                        dve.wait_ge(a_th, a * 2 + h + 1)
                        eng.scalar_tensor_tensor(g2[:, h, :], thg[:, h, :], 1.0, b(GTB[h]), ADD, MUL).then_inc(d_g2, 1)
                    for h in range(2):
                        dve.wait_ge(p_us, a * 2 + h + 1)
                        dve.wait_ge(a_v, a * 2 + h + 1)
                        dve.wait_ge(p_o, a * 2)
                        eng.tensor_tensor(uv[:, h, :], b(UB[h]), vT[:, h, :, :].rearrange("p b l -> p (b l)"), MUL).then_inc(d_uv, 1)
                    dve.wait_ge(ld_s, a * 16 + 16)

            def part_two(r, a):
                for t in range(NST):
                    if a is not None and t >= 4:
                        averages(a, t - 4)
                    if r is not None:
                        recur(r, t)
                    if a is not None:
                        maxima(a, t)
                if a is not None:
                    for t in range(NST - 4, NST):
                        averages(a, t)

            eng.memset(wS[:, :, :, 0], 0.0).then_inc(d_const, 1)
            eng.memset(mhalf[:, :], -0.5).then_inc(d_const, 1)
            eng.memset(minus[:, :], -1.0).then_inc(d_const, 1)
            for k in range(3):
                eng.memset(epst[k][:, :], (1e-5, 1e-5, 1e-6)[k]).then_inc(d_const, 1)
            dve.wait_ge(ld_v, 64)
            eng.tensor_scalar(qsc[:, :], mk[:, M_G:M_G + 4], float(S) ** -0.5, None, MUL).then_inc(d_set, 1)
            dve.wait_ge(d_set, 1)
            for h in range(2):
                eng.tensor_scalar(qbi[:, h, :], qsc[:, :], vec("bq", h), None, MUL).then_inc(d_set, 1)
                eng.tensor_scalar(kbi[:, h, :], mk[:, M_K:M_K + 4], vec("bk", h), None, MUL).then_inc(d_set, 1)
                bv = rowt[:, 3 * E:NROW].rearrange("p (k x d) -> p k x d", k=4, x=2)
                eng.tensor_scalar(bvx[:, h, :, :], bv[:, :, h, :], mk[:, M_X + h:M_X + h + 1], None, MUL).then_inc(d_set, 1)
            eng.tensor_scalar(gnh[:, :, :], vt[:, :, VI["gn_w"]:VI["gn_w"] + 2], 0.5, None, MUL).then_inc(d_set, 1)
            for i in range(2):
                eng.tensor_copy(Vd[:, :, :, i, S], mk[:, M_X + i:M_X + i + 1].unsqueeze(1).to_broadcast([P, GB, 4])).then_inc(d_set, 1)
            dve.wait_ge(d_set, 10)
            part_one(0, None, None)
            part_two(0, None)
            part_one(1, 0, None)
            part_two(1, 0)
            with dve.Fori(2, G) as g:
                part_one(g, g - 1, g - 2)
                part_two(g, g - 1)
            part_one(None, G - 1, G - 2)
            part_two(None, G - 1)
            dve.wait_ge(st_out, (G - 1) * 16)
            finish(G - 1)

        @block.tensor
        def _(pe):
            mm = nc.tensor.matmul

            def turn(k, g, src, banks, sig):
                for h in range(2):
                    for t in range(NT):
                        i = nc.tensor.transpose(bank[banks[h]][:, t * P:(t + 1) * P], src[:, t, h * P:(h + 1) * P], C(C_ID))
                    i.then_inc(sig, 1)

            def channels(o, lhs, rhs, sig, m=None):
                for kh in range(2):
                    i = mm(o, lhs(kh), rhs(kh), start=(kh == 0), stop=(kh == 1))
                i.then_inc(sig, 1)

            def full(o, name, src, h, sig):
                channels(b(o, "time"), lambda kh: W(name, kh, h * P, P), lambda kh: src[:, kh, :, :], sig)

            def tokens(o, lhs, name, sig):
                for t in range(2):
                    for kh in range(2):
                        i = mm(b(o, "token")[:, t, :], lhs(t, kh), W(name, kh), start=(kh == 0), stop=(kh == 1))
                i.then_inc(sig, 1)

            def small_products(g, first, end):
                for n in range(first, end):
                    j, h = XXX[n]
                    if n >= 4:
                        pe.wait_ge(d_tj, g * 10 + n - 3)
                    q = slice(DM * j, DM * j + DM)
                    w, a = (w2at[q, h * P:h * P + P], h1a[q, :]) if j < 4 else (w2bt[:, h * P:h * P + P], h1b[:, :])
                    mm(b(n % 4), w, a, start=True, stop=True).then_inc(p_xx, 1)

            def spread(g, t):
                if t == 0:
                    pe.wait_ge(d_g2, g * 2 + 2)
                elif t == 1:
                    pe.wait_ge(d_uv, g * 2 + 1)
                else:
                    pe.wait_ge(d_a, g * NST + t - 1)
                mm(b(t % 2, "time"), C(C_R + t % 8), vT[:, t // 8, :, :], start=True, stop=True).then_inc(p_vr, 1)

            def gather(g, t):
                h, j = divmod(t, 8)
                if j == 0:
                    pe.wait_ge(d_uv, g * 2 + h + 1)
                    if h == 0:
                        pe.wait_ge(a_hT, g * 2)
                    else:
                        pe.wait_ge(a_sq, g * 2 + 1)
                    mm(b(RO), C(C_CEN), uv[:, h, :], start=True, stop=False)
                pe.wait_ge(q_pr, g * NST + t + 1)
                i = mm(b(RO, "time"), C(C_S + j), pr[:, t % 2, :, :], start=False, stop=(j == 7))
                i.then_inc(p_rd, 1)
                if j == 7:
                    pe.wait_ge(p_rd, g * NST + t + 1)
                    pe.nop().then_inc(p_o, 1)

            def scores(g, t, r):
                bb, h = divmod(t, 2)
                if t == 0:
                    if r is not None:
                        pe.wait_ge(d_uv, r * 2 + 2)
                        pe.wait_ge(d_g2, r * 2 + 2)
                    pe.wait_ge(a_qd, g * 8 + 8)
                    pe.wait_ge(d_kd, g * 8 + 8)
                if t >= 2:
                    pe.wait_ge(d_ms, g * NST + t - 1)
                for i in range(2):
                    m = mm(bank[SCB[t % 2]][:, 256 * i:256 * i + 256], qd[:, h, bb, 2 * i:2 * i + 2, :].rearrange("p g l -> p (g l)"),
                           kd[:, h, bb, :, :].rearrange("p k s -> p (k s)"), start=True, stop=True)
                m.then_inc(p_s, 1)

            def turn_probs(g, t):
                pe.wait_ge(a_ex, g * NST + t + 1)
                if t >= 2:
                    pe.wait_ge(a_pt, g * NST + t - 1)
                for i in range(4):
                    m = nc.tensor.transpose(bank[PTB[t % 2]][:, i * P:(i + 1) * P],
                                            ex[:, t % 2, 2 * i:2 * i + 2, :].rearrange("p k s -> p (k s)"), C(C_ID))
                m.then_inc(p_pt, 1)

            def values(g, t):
                bb, h = divmod(t, 2)
                pe.wait_ge(a_pt, g * NST + t + 1)
                if t == 0:
                    pe.wait_ge(d_V, g * 2 + 2)
                if t >= 1:
                    pe.wait_ge(d_on, g * NST + t)
                for i in range(4):
                    m = mm(bank[OB][:, 18 * i:18 * i + 18], PTs[:, t % 2, 2 * i:2 * i + 2, :].rearrange("p k s -> p (k s)"),
                           Vd[:, bb, 2 * h + i % 2, :, :].rearrange("p x d -> p (x d)"), start=True, stop=True)
                m.then_inc(p_av, 1)

            def turn_output(g):
                pe.wait_ge(a_pt, g * NST + NST)
                pe.wait_ge(d_on, g * NST + NST)
                for c in range(2):
                    for i in range(4):
                        m = nc.tensor.transpose(bank[OTB[c]][:, i * P:(i + 1) * P],
                                                On[:, 4 * c + i, :, :, :].rearrange("p h k d -> p (h k d)"), C(C_ID))
                    m.then_inc(p_ot, 1)

            def project_output(g):
                for c in range(2):
                    pe.wait_ge(a_ot, g * 2 + c + 1)
                    tokens(W1B[c], lambda t, gp: cb[:, gp, 4 * c + 2 * t:4 * c + 2 * t + 2, :].rearrange("p b l -> p (b l)"), "O", p_w1)

            def tok(src, c):
                return lambda t, kh: src[:, kh, (2 * c + t) * P:(2 * c + t + 1) * P]

            def part_one(a, c, f):
                if f is not None:
                    turn_output(f)
                if c is not None:
                    pe.wait_ge(a_sq, c * 2 + 2)
                    for t in range(NT):
                        for h in range(2):
                            at = t * H + h * H // 2
                            i = mm(bank[VAR][:, at:at + H // 2], sq[:, h, t * P:(t + 1) * P], Ct[:, C_AVG:C_AVG + H // 2],
                                   start=True, stop=True)
                    i.then_inc(p_var, 1)
                if f is not None:
                    project_output(f)
                if a is not None:
                    pe.wait_ge(a_xn[0], a * NT + NT)
                    pe.wait_ge(d_a, a * NST)
                    turn(0, a, xn, XA, p_xT[0])
                if c is not None:
                    pe.wait_ge(ld_w2, 16)
                    pe.wait_ge(ld_c, c * 16 + 16)
                    if f is not None:
                        pe.wait_ge(d_x3, f * 2 + 1)
                        pe.wait_ge(a_ot, f * 2 + 2)
                    for h in range(2):
                        channels(b(KEY[h], "time"), lambda kh: W("K", kh, h * P, P), lambda kh: ct[:, kh, :, :], p_K)
                    pe.wait_ge(a_sd, c + 1)
                    for t in range(NT):
                        i = nc.tensor.transpose(bank[RGB][0:H, t * P:(t + 1) * P], rg[:, t, :], C(C_ID))
                    i.then_inc(p_rg, 1)
                if a is not None:
                    pe.wait_ge(d_xm0, a * 2 + 2)
                    if c is not None and f is not None:
                        pe.wait_ge(d_ms, a * NST - NST)
                    channels(b(H1[0], "time"), lambda kh: W("w1", kh, 0, P), lambda kh: xmx[:, kh, :, :], p_h1)
                    channels(as_time(bank[H1[1]][0:DM, :]), lambda kh: W("w1", kh, P, DM), lambda kh: xmx[:, kh, :, :], p_h1)
                if c is not None:
                    pe.wait_ge(a_rg, c + 1)
                    if f is not None:
                        pe.wait_ge(d_x3, f * 2 + 2)
                    for h in range(2):
                        mm(b(SPR[h], "time"), Ct[0:H, C_SPR + h * P:C_SPR + (h + 1) * P], cb[0:H, 0, :, :],
                           start=True, stop=True).then_inc(p_sp, 1)
                    pe.wait_ge(d_kd, c * 8 + 4)
                    for bb in range(GB):
                        for xh in range(2):
                            for kh in range(2):
                                i = mm(bank[VAL][xh * L:(xh + 1) * L, bb * L:(bb + 1) * L], ct[:, kh, bb, :], W("V", kh),
                                       start=(kh == 0), stop=(kh == 1))
                    i.then_inc(p_V, 1)
                if a is not None:
                    pe.wait_ge(a_h1, a * 2 + 2)
                    pe.wait_ge(a_xs[0], a * 2 + 2)
                    small_products(a, 0, 6)
                if c is not None:
                    pe.wait_ge(d_og, c * 2 + 2)
                    pe.wait_ge(d_kd, c * 8 + 8)
                    for i in range(2):
                        tokens(WOB[i], tok(sq, i), "Wo", p_wo)
                if a is not None:
                    small_products(a, 6, 10)
                    pe.wait_ge(q_xm, a * 10 + 6)
                    pe.wait_ge(d_tj, a * 10 + 7)
                    channels(as_time(bank[TD1][0:DD, :]), lambda kh: W("td1", kh), lambda kh: xm[1][:, kh, :, :], p_td1)
                if c is not None:
                    pe.wait_ge(a_xn[1], c * NT + NT)
                    pe.wait_ge(d_V, c * 2 + 2)
                    turn(1, c, as_tok2(oc), XB, p_xT[1])
                if a is not None:
                    pe.wait_ge(q_xm, a * 10 + 7)
                    pe.wait_ge(d_tj, a * 10 + 10)
                    channels(b(VB[0], "time"), lambda kh: W("Wv", kh, 0, P), lambda kh: xm[2][:, kh, :, :], p_v)
                    pe.wait_ge(a_hw, a + 1)
                    for h in range(2):
                        mm(b(TD2[h]), td2t[:, h * P:h * P + P], hw, start=True, stop=True).then_inc(p_td2, 1)
                    channels(b(VB[1], "time"), lambda kh: W("Wv", kh, P, P), lambda kh: xm[2][:, kh, :, :], p_v)
                if c is not None:
                    pe.wait_ge(d_mixc, c * 4 + 2)
                    pe.wait_ge(d_x1, c * 2 + 2)
                    for h in range(2):
                        channels(b(FKB[h]), lambda kh: W("Wfk", kh, h * P, P), lambda kh: oc[:, kh, :], p_fk)
                if a is not None:
                    pe.wait_ge(a_ew, a * 2 + 2)
                    for h in range(2):
                        full(KB[h], "Wk", xm[0], h, p_k)
                if c is not None:
                    pe.wait_ge(d_mixc, c * 4 + 4)
                    pe.wait_ge(a_xs[1], c * 2 + 2)
                    for i in range(2):
                        tokens(FRB[i], tok(sq, i), "Wfr", p_fr)
                if a is not None:
                    pe.wait_ge(q_xm, a * 10 + 8)
                    pe.wait_ge(a_v, a * 2 + 2)
                    for h in range(2):
                        full(RB[h], "Wr", xm[3], h, p_r)
                if c is not None:
                    pe.wait_ge(a_kk, c * 2 + 2)
                    for i in range(2):
                        tokens(FVB[i], tok(cb[:, :, :, :].rearrange("p h b l -> p h (b l)"), i), "Wfv", p_fv)
                if a is not None:
                    pe.wait_ge(q_xm, a * 10 + 10)
                    pe.wait_ge(a_k, a * 2 + 2)
                    for h in range(2):
                        full(GTB[h], "Wg", xm[4], h, p_g)
                if c is not None:
                    pe.wait_ge(d_hid, c * 2 + 2)
                    pe.wait_ge(a_tr, c * 2 + 2)
                    turn(1, c, hid, HTB, p_hT)
                if a is not None:
                    pe.wait_ge(a_r, a * 2 + 2)
                    for h in range(2):
                        pe.wait_ge(d_z, a * 2 + h + 1)
                        mm(b(UB[h], "time"), C(C_SUM), zt[:, h, :, :], start=True, stop=True).then_inc(p_us, 1)
                if c is not None:
                    pe.wait_ge(a_hT, c * 2 + 2)
                    for h in range(2):
                        channels(b(QB[h], "time"), lambda kh: W("Q", kh, h * P, P), lambda kh: cb[:, kh, :, :], p_q)

            def part_two(r, a):
                for t in range(NST + 3):
                    if t < NST:
                        if r is not None:
                            spread(r, t)
                        if a is not None:
                            scores(a, t, r)
                    if r is not None and 2 <= t < NST + 2:
                        gather(r, t - 2)
                    if a is not None and 2 <= t < NST + 2:
                        turn_probs(a, t - 2)
                    if a is not None and t >= 3:
                        values(a, t - 3)

            pe.wait_ge(ld_cn, 16)
            pe.wait_ge(ld_w, 64)
            part_one(0, None, None)
            part_two(0, None)
            part_one(1, 0, None)
            part_two(1, 0)
            with pe.Fori(2, G) as g:
                part_one(g, g - 1, g - 2)
                part_two(g, g - 1)
            part_one(None, G - 1, G - 2)
            part_two(None, G - 1)
            turn_output(G - 1)
            project_output(G - 1)


def shape_constants():
    import numpy as np
    p = np.arange(P)
    head, sub = p // S, p % S
    same = (head[:, None] == head[None, :])
    whole = np.zeros((P, C_ALL), np.float32)
    c = whole[:, :NCONST * P].reshape(P, NCONST, P)
    c[:, C_ID] = np.eye(P)
    for j in range(S):
        c[:, C_R + j] = same & (sub[:, None] == j)
        c[:, C_S + j] = same * ((sub[None, :] == j) - 1.0 / S)
    c[:, C_SUM] = same
    whole[:, C_AVG:C_AVG + H // 2] = (head[:, None] == np.arange(H // 2)[None, :]) / float(S)
    for h in range(2):
        whole[0:H, C_SPR + h * P:C_SPR + (h + 1) * P] = np.arange(H)[:, None] == head[None, :] + h * H // 2
    c[:, C_CEN] = np.eye(P) - same / float(S)
    m = np.zeros((P, NMASK), np.float32)
    for i in range(4):
        m[:, M_G + i] = (p // S) % GR == i
        m[:, M_K + i] = p // (GR * S) == i
    for i in range(2):
        m[:, M_X + i] = p // L == i
    return whole, m


def kernel(**inputs):
    import numpy as np
    import concourse.bacc as bacc
    from concourse import mybir as my
    from concourse.bass_utils import run_bass_kernel_spmd as run

    a = {k: np.asarray(v) for k, v in inputs.items()}
    l0 = {k[len("L0_xattn_"):]: v for k, v in a.items() if k.startswith("L0_xattn_")}
    l1 = {k[len("L1_xattn_"):]: v for k, v in a.items() if k.startswith("L1_xattn_")}

    def halves(w):
        return w.reshape(2, P, -1).transpose(1, 0, 2)

    ctx = a["ctx_2048"]
    wo1 = l1["Wo"].reshape(2, 4, 2, 2, S, E).transpose(3, 0, 2, 1, 4, 5).reshape(E, E)
    wk1 = np.broadcast_to(l1["Wk"].reshape(E, KVH, 1, S), (E, KVH, GR, S)).reshape(E, E)
    bk1 = np.broadcast_to(l1["bk"].reshape(KVH, 1, S), (KVH, GR, S)).reshape(E)
    w = {"w1": l0["maa_w1"], "td1": l0["td_w1"], "Wv": l0["Wv"].T, "Wk": l0["Wk"].T, "Wr": l0["Wr"].T, "Wg": l0["Wg"].T,
         "Wo": l0["Wo"].T, "Wfk": l0["Wfk"].T, "Wfr": l0["Wfr"].T, "Wfv": l0["Wfv"].T, "Q": l1["Wq"], "K": wk1,
         "V": l1["Wv"], "O": wo1}
    v = {"ln1_w": l0["ln1_w"], "ln1_b": l0["ln1_b"], "ln2_w": l0["ln2_w"], "ln2_b": l0["ln2_b"], "maa_x": l0["maa_x"],
         "decay": l0["time_decay"], "u": l0["u"].reshape(E), "gn_w": l0["gn_w"], "gn_b": l0["gn_b"],
         "fk": l0["ffn_maa_k"], "fr": l0["ffn_maa_r"], "bq": l1["bq"], "bk": bk1}
    for j in range(5):
        v[f"st{j}"] = l0["maa_stack"][0, j]
    consts, masks = shape_constants()
    arrays = {
        "x": a["x"].reshape(G, NT, P, E).transpose(0, 2, 1, 3),
        "ctxT": ctx.reshape(G, GB, L, 2, P).transpose(0, 4, 3, 1, 2),
        "srows": ctx[:, 0:2, :].reshape(G, GB, 2, 2, P).transpose(4, 2, 0, 3, 1),
        "s0": ctx[:, 2:2 + S, :].reshape(G, GB, 2, P, S).transpose(0, 3, 2, 1, 4),
        "mask": a["mask_Bx1xSxS2_ff0"].reshape(G, GB, L, L).transpose(0, 2, 1, 3),
        "wpack": np.concatenate([halves(w[n]) for n, _ in WEIGHTS], axis=2),
        "w2a": l0["maa_w2"][:4].reshape(P, E),
        "w2b": l0["maa_w2"][4],
        "td2": l0["td_w2"],
        "vecs": np.stack([v[n].reshape(2, P).T for n in VECS], axis=2),
        "consts": consts,
        "masks": masks,
        "rows": np.concatenate([l1["bo"], l1["gamma"], l1["beta"], l1["bv"]]),
    }
    arrays = {k: np.ascontiguousarray(t) for k, t in arrays.items()}
    nc = bacc.Bacc("TRN2", target_bir_lowering=False, num_devices=1)
    args = [nc.dram_tensor(k, t.shape, my.dt.from_np(t.dtype), kind="ExternalInput").ap() for k, t in arrays.items()]
    out = nc.dram_tensor("out", (G, P, NT, E), my.dt.from_np(np.dtype("float32")), kind="ExternalOutput").ap()
    xattn_kernel(nc, *args, out)
    r = run(nc, [arrays], core_ids=[0])
    return r.results[0]["out"].transpose(0, 2, 1, 3).reshape(B, L, E)
```

```python
import concourse.bass as bass
from concourse import mybir
from contextlib import ExitStack

B, L, E, H, S = 32, 64, 256, 32, 8
P = 128
GB = 8
G = B // GB
T = GB * L
NT = T // P
DM, DD = 32, 64
KVH, GR = 8, 4
NST = 16

WEIGHTS = [("w1", 5 * DM), ("td1", DD), ("Wv", E), ("Wk", E), ("Wr", E), ("Wg", E), ("Wo", E), ("Wfk", E),
           ("Wfr", E), ("Wfv", E), ("Q", E), ("K", E), ("V", KVH * S), ("O", E)]
W_AT, W_ALL = {}, 0
for _n, _w in WEIGHTS:
    W_AT[_n] = (W_ALL, _w)
    W_ALL += _w
W_MIX = W_AT["Wv"][0]
W_FIRST = W_AT["Wo"][0]
VECS = ["ln1_w", "ln1_b", "ln2_w", "ln2_b", "maa_x", "st0", "st1", "st2", "st3", "st4", "decay", "u",
        "gn_w", "gn_b", "fk", "fr", "bq", "bk"]
VI = {n: i for i, n in enumerate(VECS)}
C_ID, C_S, C_SUM, C_CEN, NCONST = 0, 1, 9, 10, 11
C_AVG = NCONST * P
C_SPR = C_AVG + H // 2
C_ALL = C_SPR + 2 * P
NPART, PQ = 3, 32
M_G, M_K, NMASK = 0, 4, 8
NCONSTS, NSET = 7, 8
NROW = 3 * E + KVH * S


def xattn_kernel(nc, x, ctxT, srows, s0_in, mask, wpack, w2a, w2b, td2, vecs, consts, ones, masks, rows, out):
    f32 = mybir.dt.float32
    bf16 = mybir.dt.bfloat16
    ALU = mybir.AluOpType
    ACT = mybir.ActivationFunctionType
    AX = mybir.AxisListType
    MUL, ADD, SUB, MAX = ALU.mult, ALU.add, ALU.subtract, ALU.max

    es = ExitStack()
    with es:
        def sb(name, shape):
            return es.enter_context(nc.sbuf_tensor(name, shape, f32))

        Wt = sb("Wt", [P, 2, W_ALL])
        w2at = sb("w2at", [P, E])
        w2bt = sb("w2bt", [DM, E])
        td2t = sb("td2t", [DD, E])
        vt = sb("vt", [P, 2, len(VECS)])
        Ct = sb("Ct", [P, C_ALL])
        mk = sb("mk", [P, NMASK])
        rowt = sb("rowt", [P, NROW])
        qsc = sb("qsc", [P, GR])
        qbi = sb("qbi", [P, 2, GR])
        kbi = sb("kbi", [P, 2, 4])
        onef = sb("onef", [NPART * PQ, 2, P])
        one = es.enter_context(nc.sbuf_tensor("one", [NPART * PQ, 2, P], bf16))
        gnh = sb("gnh", [P, 2, 2])
        mhalf = sb("mhalf", [P, NT])
        marks = sb("marks", [P, 3])
        minus = sb("minus", [P, NT])
        epst = [sb(f"epst{k}", [P, NT]) for k in range(3)]
        xt = sb("xt", [P, NT, E])
        ct = sb("ct", [P, 2, GB, L])
        s0t = sb("s0t", [P, 2, GB, S])
        mt = sb("mt", [P, GB, L])
        stats = [sb(f"stats{k}", [P, NT, 6]) for k in range(3)]
        mv = [sb(f"mv{k}", [P, NT, 2]) for k in range(3)]
        rs = [sb(f"rs{k}", [P, 4, NT]) for k in range(3)]
        xn = sb("xn", [P, NT, E])
        srow = sb("srow", [P, 2, G, 2, GB])
        xs = sb("xs", [P, 2, GB, L + 1])
        sx = sb("sx", [P, 2, GB, L])
        xmx = sb("xmx", [P, 2, GB, L])
        h1a = sb("h1a", [P, T])
        h1b = sb("h1b", [DM, T])
        tj = sb("tj", [P, 2, GB, L])
        xm = [sb(f"xm{j}", [P, 2, GB, L]) for j in range(5)]
        hw = h1a[0:DD, :]
        wS = sb("wS", [P, 2, GB, L])
        vT = sb("vT", [P, 2, GB, L])
        kT = sb("kT", [P, 2, GB, L])
        rT = sb("rT", [P, 2, GB, L])
        thg = sb("thg", [P, 2, T])
        g2 = sb("g2", [P, 2, T])
        uv = sb("uv", [P, 2, T])
        aS = sb("aS", [P, 2, GB, L])
        Sr = sb("Sr", [P, 3, GB, L])
        pr = sb("pr", [P, 2, GB, L])
        oc = sb("oc", [P, 2, T])
        sq = sb("sq", [P, 2, T])
        hid = sb("hid", [P, NT, E])
        vs = sb("vs", [P, NT, H])
        vi = sb("vi", [P, NT, H])
        rg = sb("rg", [P, NT, H])
        cb = sb("cb", [P, 2, GB, L])
        xc = sb("xc", [P, 2, GB, L + 1])
        qd = sb("qd", [P, 2, GB, GR, L])
        kd = sb("kd", [P, 2, GB, 4, L])
        Vd = sb("Vd", [P, GB, 4, 2, S + 1])
        nmx = sb("nmx", [P, 3, 8])
        ri2 = sb("ri2", [P, 2, 8])
        On = sb("On", [P, GB, 2, 8, S])
        x3 = sb("x3", [P, NT, E])
        zt = xmx
        ew = xmx
        sc, dx, ex, PTs = (xm[j] for j in range(4))
        bank = [es.enter_context(nc.psum_tensor(f"bank{i}", [P, 512], f32)) for i in range(8)]

        def b(i, kind=None):
            if kind == "time":
                return bank[i][:, :].rearrange("p (b l) -> p b l", l=L)
            if kind == "token":
                return bank[i][:, :].rearrange("p (t e) -> p t e", e=E)
            return bank[i][:, :]

        def W(n, kh, a=0, w=None):
            at, width = W_AT[n]
            return Wt[:, kh, at + a:at + a + (width if w is None else w)]

        def vec(n, h):
            return vt[:, h, VI[n]:VI[n] + 1]

        def C(i):
            return Ct[:, i * P:(i + 1) * P]

        sxf, tjf = (t[:, :, :, :].rearrange("p h b l -> p (h b l)") for t in (sx, tj))
        part = [sxf[:, 0:T].bitcast(bf16), sxf[:, T:2 * T].bitcast(bf16), tjf[:, 0:T].bitcast(bf16)]
        rest = uv
        vst = [xn[:, :, :].rearrange("p t e -> p (t e)").bitcast(bf16).rearrange("p (q n) -> p q n", n=T),
               xs[:, :, :, :].rearrange("p h b l -> p (h b l)")[:, 0:2 * T].bitcast(bf16).rearrange("p (q n) -> p q n", n=T)]

        def as_time(t):
            return t.rearrange("p (b l) -> p b l", l=L)

        def as_tokens(t):
            return t[:, :, :].rearrange("p h n -> p (h n)").rearrange("p (t e) -> p t e", e=E)

        KEY, XA, H1, TD1, TD2, VB, KB, RB, GTB, UB = (
            (2, 3), (0, 1), (0, 1), 2, (3, 0), (1, 2), (3, 0), (1, 2), (3, 0), (1, 2))
        VAL, OTB, VAR, W1B, RGB, SPR, WOB, XB, FKB, FRB, FVB, HTB, QB = (
            6, (4, 5), 7, (4, 5), 7, (6, 7), (4, 5), (6, 7), (4, 5), (6, 7), (4, 5), (6, 7), (4, 5))
        VR, SCB, PTB, OB, RO = (0, 1), (2, 3), (4, 5), 6, 7
        XXX = [(1, 0), (2, 0), (0, 0), (3, 0), (1, 1), (0, 1), (2, 1), (3, 1), (4, 0), (4, 1)]
        BY_DVE = (1, 2)

        def added(n, mine):
            return sum((j in BY_DVE) == mine for j, _ in XXX[:n])

        def sem(n):
            return es.enter_context(nc.semaphore(n))

        ld_x, ld_c, ld_s, ld_m, ld_w, ld_w2, ld_wm, ld_cn, ld_id, ld_one, ld_v, st_out = map(
            sem, "ld_x ld_c ld_s ld_m ld_w ld_w2 ld_wm ld_cn ld_id ld_one ld_v st_out".split())
        d_const, d_set, d_one = sem("d_const"), sem("d_set"), sem("d_one")
        d_bn = [sem(f"d_bn{k}") for k in range(3)]
        d_mv = [sem(f"d_mv{k}") for k in range(3)]
        q_ve = [sem(f"q_ve{k}") for k in range(3)]
        q_rs = [sem(f"q_rs{k}") for k in range(3)]
        q_mr = [sem(f"q_mr{k}") for k in range(3)]
        q_nm = [sem(f"q_nm{k}") for k in range(3)]
        a_xn = [sem(f"a_xn{k}") for k in range(3)]
        p_xT = [sem(f"p_xT{k}") for k in range(2)]
        a_xs = [sem(f"a_xs{k}") for k in range(2)]
        d_row = [sem(f"d_row{k}") for k in range(2)]
        d_sx = [sem(f"d_sx{k}") for k in range(2)]
        (d_xm0, p_h1, a_h1, p_xx, d_tj, q_xm, p_td1, a_hw, p_td2, a_ew, a_w, p_v, a_v, p_k, a_k, p_r, a_r,
         p_g, a_th, a_hi, d_lo, a_mid, q_lo, ld_vst, d_xm, d_g2, d_z, p_us, d_uv) = map(sem, (
             "d_xm0 p_h1 a_h1 p_xx d_tj q_xm p_td1 a_hw p_td2 a_ew a_w p_v a_v p_k a_k p_r a_r "
             "p_g a_th a_hi d_lo a_mid q_lo ld_vst d_xm d_g2 d_z p_us d_uv").split())
        (p_vr, d_s0, d_a, d_sc, q_pr, p_rd, p_o, a_oc, a_sq) = map(sem, "p_vr d_s0 d_a d_sc q_pr p_rd p_o a_oc a_sq".split())
        (p_var, d_vs, d_vi, a_sd, p_rg, a_rg, p_sp, d_t1, d_t2, d_og, p_wo, d_x1, d_mixc, p_fk, a_rk, a_kk, p_fr, a_tr, p_fv, d_y1,
         d_hid, q_hb, p_hT, a_hT, ld_h, p_q, a_qd, p_K, d_kd, a_kd, p_V, d_V) = map(sem, (
             "p_var d_vs d_vi a_sd p_rg a_rg p_sp d_t1 d_t2 d_og p_wo d_x1 d_mixc p_fk a_rk a_kk p_fr a_tr p_fv d_y1 "
             "d_hid q_hb p_hT a_hT ld_h p_q a_qd p_K d_kd a_kd p_V d_V").split())
        (p_s, d_ms, d_mx, q_dx, a_ex, p_pt, a_pt, p_av, d_ri2, d_on, p_ot, a_ot, p_w1, d_x3, q_fg, q_fb) = map(sem, (
            "p_s d_ms d_mx q_dx a_ex p_pt a_pt p_av d_ri2 d_on p_ot a_ot p_w1 d_x3 q_fg q_fb").split())

        block = es.enter_context(nc.Block())

        @block.sync
        def _(sp):
            def load_x(g):
                sp.dma_start(xt[:, :, :], x[bass.ds(g, 1), :, :, :].rearrange("a p t e -> (a p) t e")).then_inc(ld_x, 16)

            def load_c(g):
                sp.dma_start(ct[:, :, :, :], ctxT[bass.ds(g, 1), :, :, :, :].rearrange("a p h b l -> (a p) h b l")).then_inc(ld_c, 16)

            def load_s(g):
                sp.dma_start(s0t[:, :, :, :], s0_in[bass.ds(g, 1), :, :, :, :].rearrange("a p h b j -> (a p) h b j")).then_inc(ld_s, 16)

            def load_m(g):
                for h in range(2):
                    sp.dma_start(mt[h * L:(h + 1) * L, :, :],
                                 mask[bass.ds(g, 1), :, :, :].rearrange("a l b s -> (a l) b s")).then_inc(ld_m, 16)

            def store(g):
                sp.wait_ge(q_fb, g * NT + NT)
                sp.dma_start(out[bass.ds(g, 1), :, :, :].rearrange("a p t e -> (a p) t e"), x3[:, :, :]).then_inc(st_out, 16)

            def load_h(g):
                sp.dma_start(hid[:, :, :], x[bass.ds(g, 1), :, :, :].rearrange("a p t e -> (a p) t e")).then_inc(ld_h, 16)

            def gather_parts(g):
                sp.wait_ge(d_xm, g * 4 + 4)
                sp.wait_ge(q_xm, g * 6 + 6)
                for i, ready in enumerate((a_hi, a_mid, q_lo)):
                    sp.wait_ge(ready, g * 2 + 2)
                    if i == 0:
                        sp.wait_ge(p_xT[0], g * 2 + 2)
                    for h in range(2):
                        for e in range(2):
                            at = PQ * i + 16 * e
                            sp.dma_start(vst[h][at:at + 16, :, :], part[i][e::2, h * T:(h + 1) * T]).then_inc(ld_vst, 16)

            load_x(0)
            sp.dma_start(Ct[:, 0:P], consts[:, 0:P]).then_inc(ld_id, 16)
            sp.dma_start(vt[:, :, :], vecs).then_inc(ld_v, 16)
            sp.dma_start(srow[:, :, :, :, :], srows).then_inc(ld_v, 16)
            sp.dma_start(mk[:, :], masks).then_inc(ld_v, 16)
            sp.dma_start(rowt[:, :], rows.rearrange("(a n) -> a n", a=1).to_broadcast([P, NROW])).then_inc(ld_v, 16)
            sp.dma_start(onef[:, :, :], ones).then_inc(ld_one, 16)
            load_s(0)
            sp.dma_start(Ct[:, P:C_ALL], consts[:, P:C_ALL]).then_inc(ld_cn, 16)
            load_c(0)
            load_m(0)
            load_h(0)
            sp.wait_ge(a_xn[0], NT)
            load_x(1)
            gather_parts(0)
            sp.wait_ge(d_s0, NST)
            load_s(1)
            sp.wait_ge(p_K, 2)
            sp.wait_ge(p_V, 1)
            load_c(1)
            sp.wait_ge(a_xn[0], 2 * NT)
            load_x(2)
            gather_parts(1)
            with sp.Fori(2, G) as g:
                sp.wait_ge(a_xn[0], g * NT + NT)
                load_x(g + 1)
                sp.wait_ge(d_s0, g * NST)
                load_s(g)
                sp.wait_ge(d_ms, (g - 1) * NST)
                load_m(g - 1)
                sp.wait_ge(d_x3, (g - 1) * 2)
                load_h(g - 1)
                gather_parts(g)
                store(g - 2)
                sp.wait_ge(p_K, g * 2)
                sp.wait_ge(p_V, g)
                sp.wait_ge(st_out, (g - 1) * 16)
                load_c(g)
            sp.wait_ge(d_ms, (G - 1) * NST)
            load_m(G - 1)
            sp.wait_ge(d_x3, (G - 1) * 2)
            load_h(G - 1)
            store(G - 2)
            for t in range(0, NT, 2):
                sp.wait_ge(q_fb, (G - 1) * NT + t + 2)
                sp.dma_start(out[G - 1, :, t:t + 2, :], x3[:, t:t + 2, :]).then_inc(st_out, 16)
            sp.wait_ge(st_out, G * 16 + 16)

        @block.gpsimd
        def _(pool):
            eng = nc.gpsimd

            def rstd(k, g, half=None):
                first, end = (0, NT) if half is None else (2 * half, 2 * half + 2)
                n = g + 1 + (half or 0)
                cut = slice(first, end)
                pool.wait_ge(d_mv[k], g * NT + end)
                if k < 2:
                    pool.wait_ge(a_xn[k], g * NT)
                eng.tensor_tensor(rs[k][:, 0, cut], mv[k][:, cut, 1], epst[k][:, cut], ADD).then_inc(q_ve[k], 1)
                pool.wait_ge(q_ve[k], n)
                eng.tensor_tensor(rs[k][:, 1, cut], rs[k][:, 0, cut], mhalf[:, cut], ALU.pow).then_inc(q_rs[k], 1)
                pool.wait_ge(q_rs[k], n)
                eng.tensor_tensor(rs[k][:, 2, cut], rs[k][:, 1, cut], mv[k][:, cut, 0], MUL).then_inc(q_mr[k], 1)
                pool.wait_ge(q_mr[k], n)
                eng.tensor_tensor(rs[k][:, 3, cut], rs[k][:, 2, cut], minus[:, cut], MUL).then_inc(q_nm[k], 1)

            def add_mixes(g, first, end):
                for n in range(first, end):
                    j, h = XXX[n]
                    if j in BY_DVE:
                        continue
                    pool.wait_ge(d_tj, g * 10 + n + 1)
                    pool.wait_ge(p_g, g * 2)
                    eng.tensor_tensor(xm[j][:, h, :, :], tj[:, n % 2, :, :], xs[:, h, :, 1:L + 1], ADD).then_inc(q_xm, 1)

            def last_part(g):
                pool.wait_ge(q_xm, g * 6 + 6)
                pool.wait_ge(d_xm, g * 4 + 4)
                for h in range(2):
                    pool.wait_ge(a_mid, g * 2 + h + 1)
                    cut = slice(h * T, (h + 1) * T)
                    eng.tensor_tensor(part[2][:, cut], rest[:, h, :], part[1][:, cut], SUB).then_inc(q_lo, 1)

            def read_state(g, t):
                pool.wait_ge(d_sc, g * NST + t + 1)
                if t == 0:
                    pool.wait_ge(a_r, g * 2 + 2)
                    pool.wait_ge(p_rd, g * NST)
                if t >= 2:
                    pool.wait_ge(p_rd, g * NST + t - 1)
                eng.tensor_tensor(pr[:, t % 2, :, :], Sr[:, t % 3, :, :], rT[:, t // 8, :, :], MUL).then_inc(q_pr, 1)

            def less_max(g, t):
                pool.wait_ge(d_mx, g * NST + t + 1)
                if t >= 2:
                    pool.wait_ge(a_ex, g * NST + t - 1)
                eng.tensor_tensor(dx[:, t % 2, :, :], sc[:, t % 2, :, :],
                                  nmx[:, t % 3, :].unsqueeze(2).to_broadcast([P, 8, L]), ADD).then_inc(q_dx, 1)

            def residual(g):
                pool.wait_ge(d_hid, g * 2 + 2)
                pool.wait_ge(p_hT, g * 2 + 2)
                eng.tensor_tensor(hid[:, :, :], hid[:, :, :], rowt[:, 0:E].unsqueeze(1).to_broadcast([P, NT, E]), ADD).then_inc(q_hb, 1)

            def finish(g, tiles=range(NT)):
                for t in tiles:
                    pool.wait_ge(a_xn[2], g * NT + t + 1)
                    eng.tensor_tensor(x3[:, t, :], x3[:, t, :], rowt[:, E:2 * E], MUL).then_inc(q_fg, 1)
                    pool.wait_ge(q_fg, g * NT + t + 1)
                    eng.tensor_tensor(x3[:, t, :], x3[:, t, :], rowt[:, 2 * E:3 * E], ADD).then_inc(q_fb, 1)

            def part_one(a, c, f):
                if a is not None:
                    add_mixes(a, 0, 6)
                if c is not None:
                    rstd(1, c)
                if a is not None:
                    add_mixes(a, 6, 10)
                if f is not None:
                    rstd(2, f)
                if a is not None:
                    last_part(a)
                    rstd(0, a + 1)
                if f is not None:
                    finish(f)
                if c is not None:
                    residual(c)

            def part_two(r, a):
                for t in range(NST):
                    if r is not None:
                        read_state(r, t)
                    if a is not None:
                        less_max(a, t)

            pool.wait_ge(d_const, NCONSTS)
            rstd(0, 0)
            pool.wait_ge(ld_v, 64)
            part_one(0, None, None)
            part_two(0, None)
            part_one(1, 0, None)
            part_two(1, 0)
            with pool.Fori(2, G) as g:
                part_one(g, g - 1, g - 2)
                part_two(g, g - 1)
            part_one(None, G - 1, G - 2)
            part_two(None, G - 1)
            rstd(2, G - 1, 0)
            finish(G - 1, (0, 1))
            rstd(2, G - 1, 1)
            finish(G - 1, (2, 3))

        @block.scalar
        def _(act):
            eng = nc.scalar
            act.dma_start(Wt[:, :, 0:W_MIX], wpack[:, :, 0:W_MIX]).then_inc(ld_wm, 16)
            act.dma_start(w2at[:, :], w2a).then_inc(ld_w, 16)
            act.dma_start(w2bt[:, :], w2b).then_inc(ld_w, 16)
            act.dma_start(td2t[:, :], td2).then_inc(ld_w, 16)
            act.dma_start(Wt[:, :, W_MIX:W_FIRST], wpack[:, :, W_MIX:W_FIRST]).then_inc(ld_w, 16)
            act.dma_start(Wt[:, :, W_FIRST:W_ALL], wpack[:, :, W_FIRST:W_ALL]).then_inc(ld_w2, 16)

            def norm(k, g, dst, src, tiles=range(NT), ready=None):
                act.wait_ge(q_nm[k], g + 1 if ready is None else ready)
                for t in tiles:
                    eng.activation(dst[:, t, :], src[:, t, :], ACT.Identity, bias=rs[k][:, 3, t:t + 1],
                                   scale=rs[k][:, 1, t:t + 1]).then_inc(a_xn[k], 1)

            def affine(k, g, dst, banks):
                for h in range(2):
                    act.wait_ge(p_xT[k], g * 2 + h + 1)
                    eng.activation(dst[:, h, :, 1:L + 1], b(banks[h], "time"), ACT.Identity, bias=vec(f"ln{k + 1}_b", h),
                                   scale=vec(f"ln{k + 1}_w", h)).then_inc(a_xs[k], 1)

            def copies(g, made, sig, banks, dst):
                for h in range(2):
                    act.wait_ge(made, g * 2 + h + 1)
                    eng.activation(dst[:, h, :, :], b(banks[h], "time"), ACT.Copy).then_inc(sig, 1)

            def half_out(g, h):
                act.wait_ge(p_o, g * 2 + h + 1)
                if h == 0:
                    act.wait_ge(p_fv, g * 2)
                eng.activation(oc[:, h, :], b(RO), ACT.Copy).then_inc(a_oc, 1)
                eng.activation(sq[:, h, :], b(RO), ACT.Square).then_inc(a_sq, 1)

            def exps(g, t):
                act.wait_ge(q_dx, g * NST + t + 1)
                if t >= 2:
                    act.wait_ge(p_pt, g * NST + t - 1)
                eng.activation(ex[:, t % 2, :, :], dx[:, t % 2, :, :], ACT.Exp).then_inc(a_ex, 1)

            def probs(g, t):
                act.wait_ge(p_pt, g * NST + t + 1)
                if t >= 2:
                    act.wait_ge(p_av, g * NST + t - 1)
                eng.activation(PTs[:, t % 2, :, :], b(PTB[t % 2], "time"), ACT.Copy).then_inc(a_pt, 1)

            def turned_half(f, c, o):
                act.wait_ge(p_ot, f * 2 + c + 1)
                eng.activation(cb[:, :, 4 * c:4 * c + 4, :],
                               bank[o][:, :].rearrange("p (b g l) -> p g b l", b=4, g=2), ACT.Copy).then_inc(a_ot, 1)

            def value_parts(a):
                act.wait_ge(p_vr, a * NST)
                act.wait_ge(d_uv, a * 2)
                for h in range(2):
                    act.wait_ge(p_v, a * 2 + h + 1)
                    if h == 0:
                        act.wait_ge(d_tj, a * 10 + 10)
                    cut = slice(h * T, (h + 1) * T)
                    eng.activation(part[0][:, cut], b(VB[h]), ACT.Copy).then_inc(a_hi, 1)
                    eng.activation(vT[:, h, :, :], b(VB[h], "time"), ACT.Copy).then_inc(a_v, 1)

            def decays(a):
                act.wait_ge(d_sc, a * NST)
                for h in range(2):
                    act.wait_ge(p_td2, a * 2 + h + 1)
                    eng.activation(ew[:, h, :, :], b(TD2[h], "time"), ACT.Exp, bias=vec("decay", h)).then_inc(a_ew, 1)
                    act.wait_ge(a_ew, a * 2 + h + 1)
                    eng.activation(wS[:, h, :, 1:L], ew[:, h, :, 0:L - 1], ACT.Exp, scale=-1.0).then_inc(a_w, 1)

            def part_one(a, c, f):
                if c is not None:
                    half_out(c, 1)
                if a is not None:
                    act.wait_ge(d_xm0, a * 2)
                    act.wait_ge(q_xm, a * 6)
                    act.wait_ge(d_xm, a * 4)
                    act.wait_ge(p_vr, a * NST)
                    affine(0, a, xs, XA)
                if f is not None:
                    act.wait_ge(p_q, (f + 1) * 2)
                    for h in range(2):
                        turned_half(f, h, OTB[h])
                if c is not None:
                    act.wait_ge(d_vi, c + 1)
                    act.wait_ge(p_rg, c)
                    eng.activation(rg[:, :, :], vi[:, :, :], ACT.Sqrt).then_inc(a_sd, 1)
                if a is not None:
                    act.wait_ge(p_h1, a * 2 + 1)
                    act.wait_ge(p_td2, a * 2)
                    eng.activation(h1a[:, :], b(H1[0]), ACT.Tanh).then_inc(a_h1, 1)
                    act.wait_ge(p_h1, a * 2 + 2)
                    eng.activation(h1b[:, :], bank[H1[1]][0:DM, :], ACT.Tanh).then_inc(a_h1, 1)
                if c is not None:
                    act.wait_ge(p_rg, c + 1)
                    if f is not None:
                        act.wait_ge(p_w1, f * 2 + 2)
                    eng.activation(cb[0:H, 0, :, :], bank[RGB][0:H, :].rearrange("p (b l) -> p b l", l=L), ACT.Copy).then_inc(a_rg, 1)
                    act.wait_ge(p_s, c * NST)
                    act.wait_ge(p_K, c * 2 + 2)
                    for i in range(4):
                        eng.activation(kd[:, 1, :, i, :], b(KEY[1], "time"), ACT.Identity, bias=kbi[:, 1, i:i + 1],
                                       scale=mk[:, M_K + i:M_K + i + 1]).then_inc(a_kd, 1)
                    act.wait_ge(d_og, c * 2 + 2)
                    norm(1, c, as_tokens(oc), hid)
                if a is not None:
                    act.wait_ge(p_td1, a + 1)
                    act.wait_ge(p_xx, a * 10 + 8)
                    eng.activation(hw, bank[TD1][0:DD, :], ACT.Tanh).then_inc(a_hw, 1)
                if c is not None:
                    affine(1, c, xc, XB)
                if a is not None:
                    if c is None:
                        decays(a)
                        value_parts(a)
                    else:
                        value_parts(a)
                        decays(a)
                if c is not None:
                    act.wait_ge(d_mixc, c * 4 + 4)
                    for h in range(2):
                        act.wait_ge(p_fk, c * 2 + h + 1)
                        eng.activation(cb[:, h, :, :], b(FKB[h], "time"), ACT.Relu).then_inc(a_rk, 1)
                        act.wait_ge(a_rk, c * 2 + h + 1)
                        eng.activation(cb[:, h, :, :], cb[:, h, :, :], ACT.Square).then_inc(a_kk, 1)
                if a is not None:
                    for h in range(2):
                        act.wait_ge(d_lo, a * 2 + h + 1)
                        eng.activation(part[1][:, h * T:(h + 1) * T], rest[:, h, :], ACT.Copy).then_inc(a_mid, 1)
                if f is not None:
                    norm(2, f, x3, x3)
                if a is not None:
                    act.wait_ge(d_a, a * NST)
                    act.wait_ge(d_z, a * 2)
                    copies(a, p_k, a_k, KB, kT)
                if c is not None:
                    for i in range(2):
                        act.wait_ge(p_fr, c * 2 + i + 1)
                        eng.activation(oc[:, i, :], b(FRB[i]), ACT.Tanh, scale=0.5).then_inc(a_tr, 1)
                if a is not None:
                    act.wait_ge(q_pr, a * NST)
                    copies(a, p_r, a_r, RB, rT)
                if c is not None:
                    act.wait_ge(p_fv, c * 2 + 2)
                    for h in range(2):
                        act.wait_ge(p_hT, c * 2 + h + 1)
                        eng.activation(cb[:, h, :, :], b(HTB[h], "time"), ACT.Copy).then_inc(a_hT, 1)
                if a is not None:
                    act.wait_ge(d_g2, a * 2)
                    for h in range(2):
                        act.wait_ge(p_g, a * 2 + h + 1)
                        eng.activation(thg[:, h, :], b(GTB[h]), ACT.Tanh, scale=0.5).then_inc(a_th, 1)
                if c is not None:
                    act.wait_ge(p_s, c * NST)
                    for h in range(2):
                        act.wait_ge(p_q, c * 2 + h + 1)
                        for i in range(GR):
                            eng.activation(qd[:, h, :, i, :], b(QB[h], "time"), ACT.Identity, bias=qbi[:, h, i:i + 1],
                                           scale=qsc[:, i:i + 1]).then_inc(a_qd, 1)

            def part_two(r, a):
                for t in range(NST):
                    if a is not None:
                        if t >= 2:
                            probs(a, t - 2)
                    if r is not None and t == 9:
                        half_out(r, 0)
                    if a is not None:
                        exps(a, t)
                    if r is None and t == NST - 3:
                        act.wait_ge(p_q, G * 2)
                        turned_half(a, 0, 0)
                    if r is not None and 10 <= t < 10 + NT:
                        if t == 10:
                            act.wait_ge(p_vr, r * NST + 8)
                        norm(0, r + 1, xn, xt, [t - 10])
                if a is not None:
                    for t in range(NST - 2, NST):
                        probs(a, t)

            act.wait_ge(d_const, NCONSTS)
            norm(0, 0, xn, xt)
            act.wait_ge(d_set, NSET)
            part_one(0, None, None)
            part_two(0, None)
            part_one(1, 0, None)
            part_two(1, 0)
            with act.Fori(2, G) as g:
                part_one(g, g - 1, g - 2)
                part_two(g, g - 1)
            part_one(None, G - 1, G - 2)
            part_two(None, G - 1)
            norm(2, G - 1, x3, x3, (0, 1), G)
            turned_half(G - 1, 1, 3)
            norm(2, G - 1, x3, x3, (2, 3), G + 1)

        @block.vector
        def _(dve):
            eng = nc.vector

            def statistics(k, g, src, tiles=range(NT), ready=None):
                for t in tiles:
                    if ready is not None and t % 2 == 0:
                        dve.wait_ge(ready, g * 2 + t // 2 + 1)
                    eng.bn_stats(stats[k][:, t, :], src[:, t, :]).then_inc(d_bn[k], 1)

            def moments(k, g, tiles=range(NT)):
                dve.wait_ge(d_bn[k], g * NT + tiles[-1] + 1)
                if k < 2:
                    dve.wait_ge(q_nm[k], g)
                eng.tensor_copy(marks[:, k:k + 1], stats[k][:, tiles[-1], 0:1])
                for t in tiles:
                    eng.bn_aggr(mv[k][:, t, :], stats[k][:, t, :]).then_inc(d_mv[k], 1)

            def next_moments(g):
                dve.wait_ge(ld_x, g * 16 + 16)
                statistics(0, g, xt)
                moments(0, g)

            def state_row(k, g, src, row):
                eng.tensor_copy(src[:, :, :, 0], srow[:, row, bass.ds(g, 1), :, :].rearrange("p a h b -> p (a h) b")).then_inc(d_row[k], 1)

            def shift(k, g, h, dst, src):
                dve.wait_ge(a_xs[k], g * 2 + h + 1)
                dve.wait_ge(d_row[k], g + 1)
                eng.tensor_tensor(dst[:, h, :, :], src[:, h, :, 0:L], src[:, h, :, 1:L + 1], SUB).then_inc(d_sx[k], 1)

            def mix(k, g, h, dst, shifted, src, name, sig):
                dve.wait_ge(d_sx[k], g * 2 + h + 1)
                eng.scalar_tensor_tensor(dst, shifted[:, h, :, :], vec(name, h), src[:, h, :, 1:L + 1], MUL, ADD).then_inc(sig, 1)

            def scaled_shifts(g, first, end):
                for n in range(first, end):
                    j, h = XXX[n]
                    dve.wait_ge(p_xx, g * 10 + n + 1)
                    if n >= 2:
                        mine = XXX[n - 2][0] in BY_DVE
                        dve.wait_ge(d_xm if mine else q_xm, g * (4 if mine else 6) + added(n - 1, mine))
                    eng.scalar_tensor_tensor(tj[:, n % 2, :, :], b(n % 4, "time"), vec(f"st{j}", h), sx[:, h, :, :],
                                             ADD, MUL).then_inc(d_tj, 1)
                    if j in BY_DVE:
                        dve.wait_ge(d_tj, g * 10 + n + 1)
                        dve.wait_ge(p_g, g * 2)
                        eng.tensor_tensor(xm[j][:, h, :, :], tj[:, n % 2, :, :], xs[:, h, :, 1:L + 1], ADD).then_inc(d_xm, 1)

            def recur(g, t):
                h, j = divmod(t, 8)
                n = g * NST + t
                eng.tensor_copy(aS[:, t % 2, :, 0], s0t[:, h, :, j]).then_inc(d_s0, 1)
                dve.wait_ge(p_vr, n + 1)
                eng.tensor_tensor(aS[:, t % 2, :, 1:L], b(t % 2, "time")[:, :, 0:L - 1], kT[:, h, :, 0:L - 1], MUL).then_inc(d_a, 1)
                if t == 0:
                    dve.wait_ge(a_w, g * 2 + 2)
                    dve.wait_ge(q_pr, g * NST)
                if t >= 3:
                    dve.wait_ge(q_pr, n - 2)
                dve.wait_ge(d_a, n + 1)
                dve.wait_ge(d_s0, n + 1)
                fl = "p b l -> p (b l)"
                eng.tensor_tensor_scan(Sr[:, t % 3, :, :].rearrange(fl), wS[:, h, :, :].rearrange(fl),
                                       aS[:, t % 2, :, :].rearrange(fl), 0.0, MUL, ADD).then_inc(d_sc, 1)

            def maxima(g, t):
                n = g * NST + t
                dve.wait_ge(p_s, n + 1)
                if t == 0:
                    dve.wait_ge(ld_m, g * 32 + 32)
                if t >= 2:
                    dve.wait_ge(q_dx, n - 1)
                eng.tensor_tensor(sc[:, t % 2, :, :], b(SCB[t % 2], "time"),
                                  mt[:, t // 2, :].unsqueeze(1).to_broadcast([P, 8, L]), ADD).then_inc(d_ms, 1)
                dve.wait_ge(d_ms, n + 1)
                if t >= 3:
                    dve.wait_ge(q_dx, n - 2)
                eng.tensor_reduce(nmx[:, t % 3, :], sc[:, t % 2, :, :], AX.X, MAX, negate=True).then_inc(d_mx, 1)

            def averages(g, t):
                n = g * NST + t
                dve.wait_ge(p_av, n + 1)
                o = bank[OB][:, 0:8 * (S + 1)].rearrange("p (k d) -> p k d", d=S + 1)
                eng.reciprocal(ri2[:, t % 2, :], o[:, :, S]).then_inc(d_ri2, 1)
                dve.wait_ge(d_ri2, n + 1)
                eng.tensor_tensor(On[:, t // 2, t % 2, :, :], o[:, :, 0:S],
                                  ri2[:, t % 2, :].unsqueeze(2).to_broadcast([P, 8, S]), MUL).then_inc(d_on, 1)

            def residual(g, c, o):
                dve.wait_ge(p_w1, g * 2 + c + 1)
                dve.wait_ge(q_hb, g + 1)
                eng.tensor_tensor(x3[:, 2 * c:2 * c + 2, :], b(o, "token"), hid[:, 2 * c:2 * c + 2, :], ADD).then_inc(d_x3, 1)

            def finish(g):
                dve.wait_ge(ld_c, min_c(g))
                for c in range(2):
                    residual(g, c, W1B[c])

            def min_c(g):
                return G * 16 if isinstance(g, int) else (g + 2) * 16

            def part_one(a, c, f):
                if a is not None:
                    dve.wait_ge(p_vr, a * NST)
                    state_row(0, a, xs, 1)
                    dve.wait_ge(p_us, a * 2)
                    dve.wait_ge(a_w, a * 2)
                    for h in range(2):
                        shift(0, a, h, sx, xs)
                        mix(0, a, h, xmx[:, h, :, :], sx, xs, "maa_x", d_xm0)
                if c is not None:
                    dve.wait_ge(p_var, c + 1)
                    eng.tensor_scalar(vs[:, :, :], bank[VAR][:, 0:NT * H].rearrange("p (t k) -> p t k", k=H), 1e-5, None, ADD).then_inc(d_vs, 1)
                    dve.wait_ge(d_vs, c + 1)
                    dve.wait_ge(a_sd, c)
                    eng.reciprocal(vi[:, :, :], vs[:, :, :]).then_inc(d_vi, 1)
                    dve.wait_ge(p_s, c * NST)
                    dve.wait_ge(p_K, c * 2 + 1)
                    for i in range(4):
                        eng.tensor_scalar(kd[:, 0, :, i, :], b(KEY[0], "time"), mk[:, M_K + i:M_K + i + 1], kbi[:, 0, i:i + 1],
                                          MUL, ADD).then_inc(d_kd, 1)
                    dve.wait_ge(p_V, c + 1)
                    for i in range(2):
                        for k in range(2):
                            src = bank[VAL][i * L:(i + 1) * L, 0:NT * KVH * S].rearrange("p (t k x d) -> p t k x d", t=NT, k=4, x=2)
                            bv = rowt[i * L:(i + 1) * L, 3 * E:NROW].rearrange("p (k x d) -> p k x d", k=4, x=2)
                            eng.tensor_tensor(Vd[k * L:(k + 1) * L, i:GB:2, :, k, 0:S], src[:, :, :, k, :],
                                              bv[:, :, k, :].unsqueeze(1).to_broadcast([L, NT, 4, S]), ADD).then_inc(d_V, 1)
                if f is not None:
                    finish(f)
                if a is not None:
                    scaled_shifts(a, 0, 2)
                if c is not None:
                    for h in range(2):
                        dve.wait_ge(p_sp, c * 2 + h + 1)
                        dve.wait_ge(a_oc, c * 2 + h + 1)
                        eng.tensor_tensor(oc[:, h, :], oc[:, h, :], b(SPR[h]), MUL).then_inc(d_t1, 1)
                    for h in range(2):
                        dve.wait_ge(d_t1, c * 2 + h + 1)
                        eng.tensor_scalar(oc[:, h, :], oc[:, h, :], gnh[:, h, 0:1], gnh[:, h, 1:2], MUL, ADD).then_inc(d_t2, 1)
                    for h in range(2):
                        dve.wait_ge(d_t2, c * 2 + h + 1)
                        eng.tensor_tensor(sq[:, h, :], g2[:, h, :], oc[:, h, :], MUL).then_inc(d_og, 1)
                if a is not None:
                    scaled_shifts(a, 2, 6)
                if c is not None:
                    dve.wait_ge(ld_h, c * 16 + 16)
                    for i in range(2):
                        dve.wait_ge(p_wo, c * 2 + i + 1)
                        eng.tensor_tensor(hid[:, 2 * i:2 * i + 2, :], b(WOB[i], "token"), hid[:, 2 * i:2 * i + 2, :], ADD).then_inc(d_x1, 1)
                        statistics(1, c, hid, (2 * i, 2 * i + 1), d_x1)
                    moments(1, c)
                if a is not None:
                    scaled_shifts(a, 6, 10)
                if c is not None:
                    state_row(1, c, xc, 0)
                    for h in range(2):
                        shift(1, c, h, cb, xc)
                        mix(1, c, h, oc[:, h, :].rearrange("p (b l) -> p b l", l=L), cb, xc, "fk", d_mixc)
                    for h in range(2):
                        mix(1, c, h, sq[:, h, :].rearrange("p (b l) -> p b l", l=L), cb, xc, "fr", d_mixc)
                if f is not None:
                    statistics(2, f, x3, ready=d_x3)
                    moments(2, f)
                if a is not None:
                    for h in range(2):
                        dve.wait_ge(a_hi, a * 2 + h + 1)
                        dve.wait_ge(a_v, a * 2 + h + 1)
                        dve.wait_ge(p_o, a * 2)
                        eng.tensor_tensor(rest[:, h, :], vT[:, h, :, :].rearrange("p b l -> p (b l)"),
                                          part[0][:, h * T:(h + 1) * T], SUB).then_inc(d_lo, 1)
                    next_moments(a + 1)
                if c is not None:
                    for i in range(2):
                        dve.wait_ge(a_tr, c * 2 + i + 1)
                        dve.wait_ge(p_fv, c * 2 + i + 1)
                        eng.scalar_tensor_tensor(sq[:, i, :], oc[:, i, :], 1.0, b(FVB[i]), ADD, MUL).then_inc(d_y1, 1)
                        dve.wait_ge(d_y1, c * 2 + i + 1)
                        dve.wait_ge(a_xn[1], c * NT + 2 * i + 2)
                        eng.scalar_tensor_tensor(hid[:, 2 * i:2 * i + 2, :], sq[:, i, :].rearrange("p (t e) -> p t e", e=E), 0.5,
                                                 hid[:, 2 * i:2 * i + 2, :], MUL, ADD).then_inc(d_hid, 1)
                if a is not None:
                    dve.wait_ge(a_w, a * 2 + 2)
                    for h in range(2):
                        dve.wait_ge(a_r, a * 2 + h + 1)
                        dve.wait_ge(a_k, a * 2 + h + 1)
                        eng.scalar_tensor_tensor(zt[:, h, :, :], rT[:, h, :, :], vec("u", h), kT[:, h, :, :], MUL, MUL).then_inc(d_z, 1)
                    for h in range(2):
                        dve.wait_ge(a_th, a * 2 + h + 1)
                        eng.scalar_tensor_tensor(g2[:, h, :], thg[:, h, :], 1.0, b(GTB[h]), ADD, MUL).then_inc(d_g2, 1)
                    for h in range(2):
                        dve.wait_ge(p_us, a * 2 + h + 1)
                        dve.wait_ge(a_v, a * 2 + h + 1)
                        dve.wait_ge(q_lo, a * 2 + h + 1)
                        eng.tensor_tensor(uv[:, h, :], b(UB[h]), vT[:, h, :, :].rearrange("p b l -> p (b l)"), MUL).then_inc(d_uv, 1)
                    dve.wait_ge(ld_s, a * 16 + 16)

            def part_two(r, a):
                for t in range(NST):
                    if a is not None and t >= 4:
                        averages(a, t - 4)
                    if r is not None:
                        recur(r, t)
                    if a is not None:
                        maxima(a, t)
                    if r is None and t == NST - 1:
                        dve.wait_ge(st_out, a * 16)
                        residual(a, 0, 1)
                        statistics(2, a, x3, (0, 1), d_x3)
                        moments(2, a, (0, 1))
                if a is not None:
                    for t in range(NST - 4, NST):
                        averages(a, t)

            eng.memset(wS[:, :, :, 0], 0.0).then_inc(d_const, 1)
            eng.memset(Vd[:, :, :, :, :], 0.0).then_inc(d_const, 1)
            eng.memset(mhalf[:, :], -0.5).then_inc(d_const, 1)
            eng.memset(minus[:, :], -1.0).then_inc(d_const, 1)
            for k in range(3):
                eng.memset(epst[k][:, :], (1e-5, 1e-5, 1e-6)[k]).then_inc(d_const, 1)
            next_moments(0)
            dve.wait_ge(ld_v, 64)
            dve.wait_ge(d_const, NCONSTS)
            eng.tensor_scalar(qsc[:, :], mk[:, M_G:M_G + 4], float(S) ** -0.5, None, MUL).then_inc(d_set, 1)
            dve.wait_ge(d_set, 1)
            for h in range(2):
                eng.tensor_scalar(qbi[:, h, :], qsc[:, :], vec("bq", h), None, MUL).then_inc(d_set, 1)
                eng.tensor_scalar(kbi[:, h, :], mk[:, M_K:M_K + 4], vec("bk", h), None, MUL).then_inc(d_set, 1)
            eng.tensor_scalar(gnh[:, :, :], vt[:, :, VI["gn_w"]:VI["gn_w"] + 2], 0.5, None, MUL).then_inc(d_set, 1)
            for i in range(2):
                eng.memset(Vd[i * L:(i + 1) * L, :, :, i, S], 1.0).then_inc(d_set, 1)
            dve.wait_ge(d_set, NSET)
            part_one(0, None, None)
            dve.wait_ge(ld_one, 16)
            eng.tensor_copy(one[:, :, :], onef[:, :, :]).then_inc(d_one, 1)
            part_two(0, None)
            part_one(1, 0, None)
            part_two(1, 0)
            with dve.Fori(2, G) as g:
                part_one(g, g - 1, g - 2)
                part_two(g, g - 1)
            part_one(None, G - 1, G - 2)
            part_two(None, G - 1)
            residual(G - 1, 1, 2)
            statistics(2, G - 1, x3, (2, 3), d_x3)
            moments(2, G - 1, (2, 3))

        @block.tensor
        def _(pe):
            mm = nc.tensor.matmul

            def turn(g, src, banks, sig, ready, tiles=1):
                for t in range(NT):
                    if t % tiles == 0:
                        pe.wait_ge(ready, g * (NT // tiles) + t // tiles + 1)
                    for h in range(2):
                        i = nc.tensor.transpose(bank[banks[h]][:, t * P:(t + 1) * P], src[:, t, h * P:(h + 1) * P], C(C_ID))
                        if t == NT - 1:
                            i.then_inc(sig, 1)

            def channels(o, lhs, rhs, sig):
                for kh in range(2):
                    i = mm(o, lhs(kh), rhs(kh), start=(kh == 0), stop=(kh == 1))
                i.then_inc(sig, 1)

            def full(o, name, src, h, sig):
                channels(b(o, "time"), lambda kh: W(name, kh, h * P, P), lambda kh: src[:, kh, :, :], sig)

            def tokens(o, lhs, name, sig):
                for t in range(2):
                    for kh in range(2):
                        i = mm(b(o, "token")[:, t, :], lhs(t, kh), W(name, kh), start=(kh == 0), stop=(kh == 1))
                i.then_inc(sig, 1)

            def small_products(g, first, end):
                for n in range(first, end):
                    j, h = XXX[n]
                    if n >= 4:
                        pe.wait_ge(d_tj, g * 10 + n - 3)
                    q = slice(DM * j, DM * j + DM)
                    w, a = (w2at[q, h * P:h * P + P], h1a[q, :]) if j < 4 else (w2bt[:, h * P:h * P + P], h1b[:, :])
                    mm(b(n % 4), w, a, start=True, stop=True).then_inc(p_xx, 1)

            def spread(g, t):
                if t == 0:
                    pe.wait_ge(d_g2, g * 2 + 2)
                elif t == 1:
                    pe.wait_ge(d_uv, g * 2 + 1)
                else:
                    pe.wait_ge(d_a, g * NST + t - 1)
                if t == 0:
                    pe.wait_ge(d_one, 1)
                    pe.wait_ge(ld_vst, g * 192 + 192)
                h, j = divmod(t, 8)
                mm(b(t % 2), one[:, j % 2, :], vst[h][0:NPART * PQ, j // 2, :], start=True, stop=True).then_inc(p_vr, 1)

            def gather(g, t):
                h, j = divmod(t, 8)
                if j == 0:
                    pe.wait_ge(d_uv, g * 2 + h + 1)
                    if h == 0:
                        pe.wait_ge(a_hT, g * 2)
                    else:
                        pe.wait_ge(a_sq, g * 2 + 1)
                    mm(b(RO), C(C_CEN), uv[:, h, :], start=True, stop=False)
                pe.wait_ge(q_pr, g * NST + t + 1)
                i = mm(b(RO, "time"), C(C_S + j), pr[:, t % 2, :, :], start=False, stop=(j == 7))
                i.then_inc(p_rd, 1)
                if j == 7:
                    pe.wait_ge(p_rd, g * NST + t + 1)
                    pe.nop().then_inc(p_o, 1)

            def scores(g, t, r):
                bb, h = divmod(t, 2)
                if t == 0:
                    if r is not None:
                        pe.wait_ge(d_uv, r * 2 + 2)
                        pe.wait_ge(d_g2, r * 2 + 2)
                    pe.wait_ge(a_qd, g * 8 + 4)
                    pe.wait_ge(d_kd, g * 4 + 4)
                    pe.wait_ge(a_kd, g * 4 + 4)
                if t == 1:
                    pe.wait_ge(a_qd, g * 8 + 8)
                if t >= 2:
                    pe.wait_ge(d_ms, g * NST + t - 1)
                for i in range(2):
                    m = mm(bank[SCB[t % 2]][:, 256 * i:256 * i + 256], qd[:, h, bb, 2 * i:2 * i + 2, :].rearrange("p g l -> p (g l)"),
                           kd[:, h, bb, :, :].rearrange("p k s -> p (k s)"), start=True, stop=True)
                m.then_inc(p_s, 1)

            def turn_probs(g, t):
                pe.wait_ge(a_ex, g * NST + t + 1)
                if t >= 2:
                    pe.wait_ge(a_pt, g * NST + t - 1)
                for i in range(4):
                    m = nc.tensor.transpose(bank[PTB[t % 2]][:, i * P:(i + 1) * P],
                                            ex[:, t % 2, 2 * i:2 * i + 2, :].rearrange("p k s -> p (k s)"), C(C_ID))
                m.then_inc(p_pt, 1)

            def values(g, t):
                bb, h = divmod(t, 2)
                pe.wait_ge(a_pt, g * NST + t + 1)
                if t == 0:
                    pe.wait_ge(d_V, g * 4 + 4)
                if t >= 1:
                    pe.wait_ge(d_on, g * NST + t)
                for i in range(4):
                    m = mm(bank[OB][:, 18 * i:18 * i + 18], PTs[:, t % 2, 2 * i:2 * i + 2, :].rearrange("p k s -> p (k s)"),
                           Vd[:, bb, 2 * h + i % 2, :, :].rearrange("p x d -> p (x d)"), start=True, stop=True)
                m.then_inc(p_av, 1)

            def turn_half(g, c, o):
                pe.wait_ge(d_on, g * NST + NST // 2 * (c + 1))
                for i in range(4):
                    m = nc.tensor.transpose(bank[o][:, i * P:(i + 1) * P],
                                            On[:, 4 * c + i, :, :, :].rearrange("p h k d -> p (h k d)"), C(C_ID))
                m.then_inc(p_ot, 1)

            def project_half(g, c, o):
                pe.wait_ge(a_ot, g * 2 + c + 1)
                tokens(o, lambda t, gp: cb[:, gp, 4 * c + 2 * t:4 * c + 2 * t + 2, :].rearrange("p b l -> p (b l)"), "O", p_w1)

            def turn_output(g):
                pe.wait_ge(a_pt, g * NST + NST)
                for c in range(2):
                    turn_half(g, c, OTB[c])

            def project_output(g):
                for c in range(2):
                    project_half(g, c, W1B[c])

            def tok(src, c):
                return lambda t, kh: src[:, kh, (2 * c + t) * P:(2 * c + t + 1) * P]

            def turn_input(g):
                pe.wait_ge(d_a, g * NST)
                turn(g, xn, XA, p_xT[0], a_xn[0])

            def keys(g, h, a):
                pe.wait_ge(ld_c, g * 16 + 16)
                if a is None:
                    pe.wait_ge(ld_w2, 16)
                else:
                    pe.wait_ge(d_ms, (a + 1) * NST)
                channels(b(KEY[h], "time"), lambda kh: W("K", kh, h * P, P), lambda kh: ct[:, kh, :, :], p_K)

            def part_one(a, c, f):
                if c is not None:
                    if f is not None:
                        pe.wait_ge(d_on, (f + 1) * NST)
                    for t in range(NT):
                        for kh in range(2):
                            i = mm(bank[VAL][:, t * KVH * S:(t + 1) * KVH * S],
                                   ct[:, kh, 2 * t:2 * t + 2, :].rearrange("p b l -> p (b l)"), W("V", kh), start=(kh == 0), stop=(kh == 1))
                    i.then_inc(p_V, 1)
                if f is not None:
                    turn_output(f)
                if c is not None:
                    pe.wait_ge(a_sq, c * 2 + 2)
                    for t in range(NT):
                        for h in range(2):
                            at = t * H + h * H // 2
                            i = mm(bank[VAR][:, at:at + H // 2], sq[:, h, t * P:(t + 1) * P], Ct[:, C_AVG:C_AVG + H // 2],
                                   start=True, stop=True)
                    i.then_inc(p_var, 1)
                if a is not None:
                    pe.wait_ge(d_xm0, a * 2 + 2)
                    pe.wait_ge(a_xs[0], a * 2 + 2)
                    if c is None:
                        pe.wait_ge(ld_wm, 16)
                    channels(b(H1[0], "time"), lambda kh: W("w1", kh, 0, P), lambda kh: xmx[:, kh, :, :], p_h1)
                    channels(as_time(bank[H1[1]][0:DM, :]), lambda kh: W("w1", kh, P, DM), lambda kh: xmx[:, kh, :, :], p_h1)
                if f is not None:
                    project_output(f)
                if c is not None:
                    pe.wait_ge(a_sd, c + 1)
                    for t in range(NT):
                        i = nc.tensor.transpose(bank[RGB][0:H, t * P:(t + 1) * P], rg[:, t, :], C(C_ID))
                    i.then_inc(p_rg, 1)
                if a is not None:
                    pe.wait_ge(a_h1, a * 2 + 2)
                    if c is None:
                        pe.wait_ge(ld_w, 64)
                    small_products(a, 0, 2)
                if c is not None:
                    pe.wait_ge(a_rg, c + 1)
                    pe.wait_ge(d_V, c * 4 + 4)
                    for h in range(2):
                        mm(b(SPR[h], "time"), Ct[0:H, C_SPR + h * P:C_SPR + (h + 1) * P], cb[0:H, 0, :, :],
                           start=True, stop=True).then_inc(p_sp, 1)
                if a is not None:
                    if c is not None:
                        pe.wait_ge(d_kd, c * 4 + 4)
                        pe.wait_ge(a_kd, c * 4 + 4)
                    small_products(a, 2, 6)
                if c is not None:
                    pe.wait_ge(d_og, c * 2 + 2)
                    if f is not None:
                        pe.wait_ge(d_x3, f * 2 + 2)
                    for i in range(2):
                        tokens(WOB[i], tok(sq, i), "Wo", p_wo)
                if a is not None:
                    small_products(a, 6, 10)
                    pe.wait_ge(d_xm, a * 4 + 3)
                    pe.wait_ge(d_tj, a * 10 + 7)
                    channels(as_time(bank[TD1][0:DD, :]), lambda kh: W("td1", kh), lambda kh: xm[1][:, kh, :, :], p_td1)
                if c is not None:
                    pe.wait_ge(d_t1, c * 2 + 2)
                    turn(c, as_tokens(oc), XB, p_xT[1], a_xn[1])
                if a is not None:
                    pe.wait_ge(d_xm, a * 4 + 4)
                    pe.wait_ge(d_tj, a * 10 + 10)
                    channels(b(VB[0], "time"), lambda kh: W("Wv", kh, 0, P), lambda kh: xm[2][:, kh, :, :], p_v)
                    pe.wait_ge(a_hw, a + 1)
                    for h in range(2):
                        mm(b(TD2[h]), td2t[:, h * P:h * P + P], hw, start=True, stop=True).then_inc(p_td2, 1)
                    channels(b(VB[1], "time"), lambda kh: W("Wv", kh, P, P), lambda kh: xm[2][:, kh, :, :], p_v)
                if c is not None:
                    pe.wait_ge(d_x1, c * 2 + 2)
                    for kh in range(2):
                        pe.wait_ge(d_mixc, c * 4 + kh + 1)
                        for h in range(2):
                            i = mm(b(FKB[h]), W("Wfk", kh, h * P, P), oc[:, kh, :], start=(kh == 0), stop=(kh == 1))
                            if kh == 1:
                                i.then_inc(p_fk, 1)
                if a is not None:
                    pe.wait_ge(a_ew, a * 2 + 2)
                    pe.wait_ge(q_xm, a * 6 + 4)
                    for h in range(2):
                        full(KB[h], "Wk", xm[0], h, p_k)
                if c is not None:
                    pe.wait_ge(d_mixc, c * 4 + 4)
                    pe.wait_ge(a_xs[1], c * 2 + 2)
                    for i in range(2):
                        tokens(FRB[i], tok(sq, i), "Wfr", p_fr)
                    pe.wait_ge(a_kk, c * 2 + 2)
                    for i in range(2):
                        tokens(FVB[i], tok(cb[:, :, :, :].rearrange("p h b l -> p h (b l)"), i), "Wfv", p_fv)
                if a is not None:
                    pe.wait_ge(a_v, a * 2 + 2)
                    for h in range(2):
                        full(RB[h], "Wr", xm[3], h, p_r)
                if c is not None:
                    pe.wait_ge(a_tr, c * 2 + 2)
                    turn(c, hid, HTB, p_hT, d_hid, 2)
                if a is not None:
                    pe.wait_ge(q_xm, a * 6 + 6)
                    pe.wait_ge(a_k, a * 2 + 2)
                    for h in range(2):
                        full(GTB[h], "Wg", xm[4], h, p_g)
                if c is not None:
                    pe.wait_ge(a_hT, c * 2 + 2)
                    for h in range(2):
                        channels(b(QB[h], "time"), lambda kh: W("Q", kh, h * P, P), lambda kh: cb[:, kh, :, :], p_q)
                if a is not None:
                    pe.wait_ge(a_r, a * 2 + 2)
                    for h in range(2):
                        pe.wait_ge(d_z, a * 2 + h + 1)
                        if c is None:
                            pe.wait_ge(ld_cn, 16)
                        mm(b(UB[h], "time"), C(C_SUM), zt[:, h, :, :], start=True, stop=True).then_inc(p_us, 1)

            def part_two(r, a):
                for t in range(NST + 3):
                    if t < NST:
                        if r is not None:
                            spread(r, t)
                        if a is not None:
                            scores(a, t, r)
                    elif r is not None:
                        if t == NST:
                            turn_input(r + 1)
                        else:
                            keys(r, t - NST - 1, a)
                    if a is not None and 2 <= t < NST + 2:
                        turn_probs(a, t - 2)
                    if r is not None and 2 <= t < NST + 2:
                        gather(r, t - 2)
                    if a is not None and t >= 3:
                        values(a, t - 3)
                    if r is None and t == NST - 4:
                        turn_half(a, 0, 0)
                    if r is None and t == NST - 2:
                        project_half(a, 0, 1)

            pe.wait_ge(ld_id, 16)
            turn_input(0)
            part_one(0, None, None)
            part_two(0, None)
            part_one(1, 0, None)
            part_two(1, 0)
            with pe.Fori(2, G) as g:
                part_one(g, g - 1, g - 2)
                part_two(g, g - 1)
            part_one(None, G - 1, G - 2)
            part_two(None, G - 1)
            turn_half(G - 1, 1, 3)
            project_half(G - 1, 1, 2)


def shape_constants():
    import numpy as np
    p = np.arange(P)
    head, sub = p // S, p % S
    same = (head[:, None] == head[None, :])
    whole = np.zeros((P, C_ALL), np.float32)
    c = whole[:, :NCONST * P].reshape(P, NCONST, P)
    c[:, C_ID] = np.eye(P)
    for j in range(S):
        c[:, C_S + j] = same * ((sub[None, :] == j) - 1.0 / S)
    c[:, C_SUM] = same
    whole[:, C_AVG:C_AVG + H // 2] = (head[:, None] == np.arange(H // 2)[None, :]) / float(S)
    for h in range(2):
        whole[0:H, C_SPR + h * P:C_SPR + (h + 1) * P] = np.arange(H)[:, None] == head[None, :] + h * H // 2
    c[:, C_CEN] = np.eye(P) - same / float(S)
    m = np.zeros((P, NMASK), np.float32)
    for i in range(4):
        m[:, M_G + i] = (p // S) % GR == i
        m[:, M_K + i] = p // (GR * S) == i
    one = np.zeros((NPART, PQ, 2, P), np.float32)
    for i in range(2):
        for k in range(H // 2):
            one[:, 16 * i + k, i, k * S:(k + 1) * S] = 1.0
    return whole, one.reshape(NPART * PQ, 2, P), m


def kernel(**inputs):
    import numpy as np
    import concourse.bacc as bacc
    from concourse import mybir as my
    from concourse.bass_utils import run_bass_kernel_spmd as run

    a = {k: np.asarray(v) for k, v in inputs.items()}
    l0 = {k[len("L0_xattn_"):]: v for k, v in a.items() if k.startswith("L0_xattn_")}
    l1 = {k[len("L1_xattn_"):]: v for k, v in a.items() if k.startswith("L1_xattn_")}

    def halves(w):
        return w.reshape(2, P, -1).transpose(1, 0, 2)

    ctx = a["ctx_2048"]
    wo1 = l1["Wo"].reshape(2, 4, 2, 2, S, E).transpose(3, 0, 2, 1, 4, 5).reshape(E, E)
    wk1 = np.broadcast_to(l1["Wk"].reshape(E, KVH, 1, S), (E, KVH, GR, S)).reshape(E, E)
    bk1 = np.broadcast_to(l1["bk"].reshape(KVH, 1, S), (KVH, GR, S)).reshape(E)
    w = {"w1": l0["maa_w1"], "td1": l0["td_w1"], "Wv": l0["Wv"].T, "Wk": l0["Wk"].T, "Wr": l0["Wr"].T, "Wg": l0["Wg"].T,
         "Wo": l0["Wo"].T, "Wfk": l0["Wfk"].T, "Wfr": l0["Wfr"].T, "Wfv": l0["Wfv"].T, "Q": l1["Wq"], "K": wk1,
         "V": l1["Wv"], "O": wo1}
    v = {"ln1_w": l0["ln1_w"], "ln1_b": l0["ln1_b"], "ln2_w": l0["ln2_w"], "ln2_b": l0["ln2_b"], "maa_x": l0["maa_x"],
         "decay": l0["time_decay"], "u": l0["u"].reshape(E), "gn_w": l0["gn_w"], "gn_b": l0["gn_b"],
         "fk": l0["ffn_maa_k"], "fr": l0["ffn_maa_r"], "bq": l1["bq"], "bk": bk1}
    for j in range(5):
        v[f"st{j}"] = l0["maa_stack"][0, j]
    consts, ones, masks = shape_constants()
    arrays = {
        "x": np.concatenate([a["x"], a["x"][:GB]]).reshape(G + 1, NT, P, E).transpose(0, 2, 1, 3),
        "ctxT": ctx.reshape(G, GB, L, 2, P).transpose(0, 4, 3, 1, 2),
        "srows": ctx[:, 0:2, :].reshape(G, GB, 2, 2, P).transpose(4, 2, 0, 3, 1),
        "s0": ctx[:, 2:2 + S, :].reshape(G, GB, 2, P, S).transpose(0, 3, 2, 1, 4),
        "mask": a["mask_Bx1xSxS2_ff0"].reshape(G, GB, L, L).transpose(0, 2, 1, 3),
        "wpack": np.concatenate([halves(w[n]) for n, _ in WEIGHTS], axis=2),
        "w2a": l0["maa_w2"][:4].reshape(P, E),
        "w2b": l0["maa_w2"][4],
        "td2": l0["td_w2"],
        "vecs": np.stack([v[n].reshape(2, P).T for n in VECS], axis=2),
        "consts": consts,
        "ones": ones,
        "masks": masks,
        "rows": np.concatenate([l1["bo"], l1["gamma"], l1["beta"], l1["bv"]]),
    }
    arrays = {k: np.ascontiguousarray(t) for k, t in arrays.items()}
    nc = bacc.Bacc("TRN2", target_bir_lowering=False, num_devices=1)
    args = [nc.dram_tensor(k, t.shape, my.dt.from_np(t.dtype), kind="ExternalInput").ap() for k, t in arrays.items()]
    out = nc.dram_tensor("out", (G, P, NT, E), my.dt.from_np(np.dtype("float32")), kind="ExternalOutput").ap()
    xattn_kernel(nc, *args, out)
    r = run(nc, [arrays], core_ids=[0])
    return r.results[0]["out"].transpose(0, 2, 1, 3).reshape(B, L, E)
```
